# Optimizing a Trainium2 kernel written in Bass

```python
import numpy as np
import jax
import jax.numpy as jnp

def _softmax(x, axis=-1):
    return jax.nn.softmax(x, axis=axis)

def _gelu(x):
    return jax.nn.gelu(x, approximate=True)

def _silu(x):
    return jax.nn.silu(x)

def _sigmoid(x):
    return jax.nn.sigmoid(x)

def _layernorm(x, axis=-1, eps=1e-05):
    m = jnp.mean(x, axis=axis, keepdims=True)
    v = jnp.var(x, axis=axis, keepdims=True)
    return (x - m) / jnp.sqrt(v + eps)

def _scatter_add(tgt, idx, src, axis=0):
    return tgt.at[idx].add(src)

def _segment_sum(src, seg, n):
    return jax.ops.segment_sum(src, seg, n)
kernel_name = 'mk_gnn_resnorm_d4_gnn_r64_a70ec1'

def setup_inputs(seed: int=0):
    np.random.seed(seed)
    _w = jnp.asarray

    def _rec_inputs():
        import jax
        import jax.numpy as jnp
        _gk = jax.random.key(seed)
        x = -0.0003713 + 1 * jax.random.normal(jax.random.fold_in(_gk, 1), (100000, 128), jnp.float32)
        src = jax.random.randint(jax.random.fold_in(_gk, 2), (25000,), 0, 100000, jnp.int32)
        dst = jax.random.randint(jax.random.fold_in(_gk, 3), (25000,), 0, 100000, jnp.int32)
        _o = jnp.argsort(dst, stable=True)
        src = src[_o]
        dst = dst[_o]
        edge_type_3 = jax.random.randint(jax.random.fold_in(_gk, 13), (25000,), 0, 3, jnp.int32)
        return (x, src, dst, edge_type_3)
    x, src, dst, edge_type_3 = _rec_inputs()

    def _L0_gnn_setup():
        import jax, jax.numpy as jnp
        import numpy as np
        N = 100000
        E = 9375
        D_IN = 128
        D_OUT = 128
        key = jax.random.key(seed)
        k1, k2, k3, k4 = jax.random.split(key, 4)
        H = jax.random.normal(k1, (N, D_IN), dtype=jnp.float32)
        edge_index = jax.random.randint(k2, (2, E), 0, N, dtype=jnp.int64)
        bound = 1.0 / np.sqrt(D_IN)
        W = jax.random.uniform(k3, (D_OUT, D_IN), minval=-bound, maxval=bound, dtype=jnp.float32)
        b = jax.random.uniform(k4, (D_OUT,), minval=-bound, maxval=bound, dtype=jnp.float32)
        return {'H': H, 'edge_index': edge_index, 'W': W, 'b': b}
    _L0_gnn_all = _L0_gnn_setup()
    _L0_gnn_in = {k: v for k, v in _L0_gnn_all.items() if k in ('W', 'b')}
    del _L0_gnn_all

    def _L1_gnn_setup():
        import jax, jax.numpy as jnp
        import numpy as np
        N = 100000
        E = 25000
        D_IN = 128
        D_HID = 128
        D_OUT = 128

        def gcn_conv(x, W, b, src, dst, n):
            h = x @ W
            deg = jax.ops.segment_sum(jnp.ones_like(dst, dtype=h.dtype), dst, num_segments=n)
            dinv = jnp.where(deg > 0, jax.lax.rsqrt(deg), 0.0)
            norm = dinv[src] * dinv[dst]
            msg = h[src] * norm[:, None]
            agg = jax.ops.segment_sum(msg, dst, num_segments=n)
            return agg + b
        key = jax.random.key(seed)
        k1, k2, k3, k4 = jax.random.split(key, 4)
        x_piece = jax.random.normal(k1, (N, D_IN), dtype=jnp.float32)
        edge_index_piece = jax.random.randint(k2, (2, E), 0, N, dtype=jnp.int64)
        W1 = jax.random.normal(k3, (D_IN, D_HID), dtype=jnp.float32) / np.sqrt(D_IN)
        b1 = jnp.zeros((D_HID,), dtype=jnp.float32)
        W2 = jax.random.normal(k4, (D_HID, D_OUT), dtype=jnp.float32) / np.sqrt(D_HID)
        b2 = jnp.zeros((D_OUT,), dtype=jnp.float32)
        return {'x_piece': x_piece, 'edge_index_piece': edge_index_piece, 'W1': W1, 'b1': b1, 'W2': W2, 'b2': b2}
    _L1_gnn_all = _L1_gnn_setup()
    _L1_gnn_in = {k: v for k, v in _L1_gnn_all.items() if k in ('W1', 'b1', 'W2', 'b2')}
    del _L1_gnn_all

    def _L2_gnn_setup():
        import jax, jax.numpy as jnp
        import numpy as np
        N_NODES = 100000
        N_EDGES = 50000
        IN_FEATS = 128
        HIDDEN = 128
        BN_EPS = 1e-05
        LEAKY_SLOPE = 0.01
        key = jax.random.key(seed)
        k1, k2, k3, k4 = jax.random.split(key, 4)
        feat = jax.random.normal(k1, (N_NODES, IN_FEATS), dtype=jnp.float32)
        W = jax.random.normal(k2, (IN_FEATS, HIDDEN), dtype=jnp.float32) * (1.0 / np.sqrt(IN_FEATS))
        b = jnp.zeros((HIDDEN,), dtype=jnp.float32)
        gamma = jnp.ones((HIDDEN,), dtype=jnp.float32)
        beta = jnp.zeros((HIDDEN,), dtype=jnp.float32)
        src = jax.random.randint(k3, (N_EDGES,), 0, N_NODES, dtype=jnp.int64)
        dst = jax.random.randint(k4, (N_EDGES,), 0, N_NODES, dtype=jnp.int64)
        return {'feat': feat, 'W': W, 'b': b, 'gamma': gamma, 'beta': beta, 'src': src, 'dst': dst}
    _L2_gnn_all = _L2_gnn_setup()
    _L2_gnn_in = {k: v for k, v in _L2_gnn_all.items() if k in ('W', 'b', 'gamma', 'beta')}
    del _L2_gnn_all

    def _L3_gnn_setup():
        import jax, jax.numpy as jnp
        import numpy as np
        N_NODES = 50000
        N_EDGES = 9375
        DIM = 128
        N_REL = 3
        LN_EPS = 1e-05
        key = jax.random.key(seed)
        ks = jax.random.split(key, 8)
        x = jax.random.normal(ks[0], (N_NODES, DIM), dtype=jnp.float32)
        edge_index = jax.random.randint(ks[1], (2, N_EDGES), 0, N_NODES, dtype=jnp.int64)
        edge_type = jax.random.randint(ks[2], (N_EDGES,), 0, N_REL, dtype=jnp.int64)
        relation_weights = jax.random.normal(ks[3], (N_REL, DIM, DIM), dtype=jnp.float32)
        lim = 1.0 / np.sqrt(DIM)
        lin_w = jax.random.uniform(ks[4], (DIM, DIM), dtype=jnp.float32, minval=-lim, maxval=lim)
        lin_b = jax.random.uniform(ks[5], (DIM,), dtype=jnp.float32, minval=-lim, maxval=lim)
        ln_gamma = jnp.ones((DIM,), dtype=jnp.float32)
        ln_beta = jnp.zeros((DIM,), dtype=jnp.float32)
        return {'x': x, 'edge_index': edge_index, 'edge_type': edge_type, 'relation_weights': relation_weights, 'lin_w': lin_w, 'lin_b': lin_b, 'ln_gamma': ln_gamma, 'ln_beta': ln_beta}
    _L3_gnn_all = _L3_gnn_setup()
    _L3_gnn_in = {k: v for k, v in _L3_gnn_all.items() if k in ('relation_weights', 'lin_w', 'lin_b', 'ln_gamma', 'ln_beta')}
    del _L3_gnn_all
    return {'x': x, 'src': src, 'dst': dst, 'edge_type_3': edge_type_3, 'L0_gnn_W': _L0_gnn_in['W'], 'L0_gnn_b': _L0_gnn_in['b'], 'L1_gnn_W1': _L1_gnn_in['W1'], 'L1_gnn_b1': _L1_gnn_in['b1'], 'L1_gnn_W2': _L1_gnn_in['W2'], 'L1_gnn_b2': _L1_gnn_in['b2'], 'L2_gnn_W': _L2_gnn_in['W'], 'L2_gnn_b': _L2_gnn_in['b'], 'L2_gnn_gamma': _L2_gnn_in['gamma'], 'L2_gnn_beta': _L2_gnn_in['beta'], 'L3_gnn_relation_weights': _L3_gnn_in['relation_weights'], 'L3_gnn_lin_w': _L3_gnn_in['lin_w'], 'L3_gnn_lin_b': _L3_gnn_in['lin_b'], 'L3_gnn_ln_gamma': _L3_gnn_in['ln_gamma'], 'L3_gnn_ln_beta': _L3_gnn_in['ln_beta']}

def reference(x, src, dst, edge_type_3, L0_gnn_W, L0_gnn_b, L1_gnn_W1, L1_gnn_b1, L1_gnn_W2, L1_gnn_b2, L2_gnn_W, L2_gnn_b, L2_gnn_gamma, L2_gnn_beta, L3_gnn_relation_weights, L3_gnn_lin_w, L3_gnn_lin_b, L3_gnn_ln_gamma, L3_gnn_ln_beta):
    import jax
    import jax.numpy as jnp

    def _L0_gnn_ref(H, edge_index, W, b):
        import jax, jax.numpy as jnp
        import numpy as np
        N = 100000
        E = 9375
        D_IN = 128
        D_OUT = 128
        n = H.shape[0]
        loops = jnp.arange(n, dtype=edge_index.dtype)
        row = jnp.concatenate([edge_index[0], loops])
        col = jnp.concatenate([edge_index[1], loops])
        deg = jax.ops.segment_sum(jnp.ones_like(row, dtype=H.dtype), row, num_segments=n)
        deg_inv_sqrt = jnp.where(deg > 0, jax.lax.rsqrt(jnp.maximum(deg, 1.0)), 0.0)
        norm = deg_inv_sqrt[row] * deg_inv_sqrt[col]
        Hl = H @ W.T + b
        msg = Hl[col] * norm[:, None]
        out = jax.ops.segment_sum(msg, row, num_segments=n)
        return jax.nn.relu(out)

    def _L1_gnn_ref(x_piece, edge_index_piece, W1, b1, W2, b2):
        import jax, jax.numpy as jnp
        import numpy as np
        N = 100000
        E = 25000
        D_IN = 128
        D_HID = 128
        D_OUT = 128

        def gcn_conv(x, W, b, src, dst, n):
            h = x @ W
            deg = jax.ops.segment_sum(jnp.ones_like(dst, dtype=h.dtype), dst, num_segments=n)
            dinv = jnp.where(deg > 0, jax.lax.rsqrt(deg), 0.0)
            norm = dinv[src] * dinv[dst]
            msg = h[src] * norm[:, None]
            agg = jax.ops.segment_sum(msg, dst, num_segments=n)
            return agg + b
        n = x_piece.shape[0]
        loops = jnp.arange(n, dtype=edge_index_piece.dtype)
        src = jnp.concatenate([edge_index_piece[0], loops])
        dst = jnp.concatenate([edge_index_piece[1], loops])
        h = gcn_conv(x_piece, W1, b1, src, dst, n)
        h = jax.nn.relu(h)
        out = gcn_conv(h, W2, b2, src, dst, n)
        return out

    def _L2_gnn_ref(feat, W, b, gamma, beta, src, dst):
        import jax, jax.numpy as jnp
        import numpy as np
        N_NODES = 100000
        N_EDGES = 50000
        IN_FEATS = 128
        HIDDEN = 128
        BN_EPS = 1e-05
        LEAKY_SLOPE = 0.01
        N = feat.shape[0]
        loop = jnp.arange(N, dtype=src.dtype)
        s = jnp.concatenate([src, loop])
        d = jnp.concatenate([dst, loop])
        ones = jnp.ones(s.shape[0], dtype=feat.dtype)
        deg_out = jnp.maximum(jax.ops.segment_sum(ones, s, num_segments=N), 1.0)
        deg_in = jnp.maximum(jax.ops.segment_sum(ones, d, num_segments=N), 1.0)
        h = feat * jax.lax.rsqrt(deg_out)[:, None]
        h = h @ W
        agg = jax.ops.segment_sum(h[s], d, num_segments=N)
        h = agg * jax.lax.rsqrt(deg_in)[:, None] + b
        mean = jnp.mean(h, axis=0)
        var = jnp.mean(jnp.square(h - mean), axis=0)
        hn = (h - mean) * jax.lax.rsqrt(var + BN_EPS) * gamma + beta
        return jnp.where(hn > 0, hn, LEAKY_SLOPE * hn)

    def _L3_gnn_ref(x, edge_index, edge_type, relation_weights, lin_w, lin_b, ln_gamma, ln_beta):
        import jax, jax.numpy as jnp
        import numpy as np
        N_NODES = 50000
        N_EDGES = 9375
        DIM = 128
        N_REL = 3
        LN_EPS = 1e-05
        N = x.shape[0]
        src, dst = (edge_index[0], edge_index[1])
        xs = x[src]
        msg = jnp.zeros_like(xs)
        for r in range(relation_weights.shape[0]):
            mask = (edge_type == r)[:, None]
            msg = msg + jnp.where(mask, xs @ relation_weights[r], jnp.zeros((), x.dtype))
        agg = jax.ops.segment_sum(msg, dst, num_segments=N)
        deg = jax.ops.segment_sum(jnp.ones_like(dst, dtype=x.dtype), dst, num_segments=N)
        deg = jnp.maximum(deg, 1.0)
        out = agg / deg[:, None]
        h = x @ lin_w.T + lin_b + out
        mu = jnp.mean(h, axis=-1, keepdims=True)
        var = jnp.mean((h - mu) ** 2, axis=-1, keepdims=True)
        return ln_gamma * (h - mu) * jax.lax.rsqrt(var + LN_EPS) + ln_beta
    edge_index = jnp.stack([src, dst])
    x = _layernorm(x + _L0_gnn_ref(x, edge_index, L0_gnn_W, L0_gnn_b), axis=-1)
    x = _layernorm(x + _L1_gnn_ref(x, edge_index, L1_gnn_W1, L1_gnn_b1, L1_gnn_W2, L1_gnn_b2), axis=-1)
    x = _layernorm(x + _L2_gnn_ref(x, L2_gnn_W, L2_gnn_b, L2_gnn_gamma, L2_gnn_beta, src, dst), axis=-1)
    x = _layernorm(x + _L3_gnn_ref(x, edge_index, edge_type_3, L3_gnn_relation_weights, L3_gnn_lin_w, L3_gnn_lin_b, L3_gnn_ln_gamma, L3_gnn_ln_beta), axis=-1)
    return x

_drawn_inputs = setup_inputs


def setup_inputs(seed=0):
    import zlib

    import numpy as np

    out = dict(_drawn_inputs(seed))
    spreads = {'L1_gnn_b1': (0.0, 0.1),
     'L1_gnn_b2': (0.0, 0.1),
     'L2_gnn_b': (0.0, 0.1),
     'L2_gnn_gamma': (1.0, 0.2),
     'L2_gnn_beta': (0.0, 0.1),
     'L3_gnn_ln_gamma': (1.0, 0.2),
     'L3_gnn_ln_beta': (0.0, 0.1)}
    factors = {}
    for name, (base, spread) in spreads.items():
        noise = np.random.default_rng([zlib.crc32(name.encode()), seed]).standard_normal(out[name].shape)
        drawn = base * np.exp(spread * noise) if base else spread * noise
        out[name] = jnp.asarray(drawn.astype(out[name].dtype))
    for name, factor in factors.items():
        out[name] = (out[name] * factor).astype(out[name].dtype)
    return out
```

```python
import numpy as np
import concourse.bass as bass
from concourse import mybir
from concourse.alu_op_type import AluOpType as ALU
from contextlib import ExitStack

F32 = mybir.dt.float32
F16 = mybir.dt.float16
I32 = mybir.dt.int32
ACT = mybir.ActivationFunctionType

P = 128
N = 100000
D = 128
E = 25000
R = 3
G = 8
B = P * G
NB = -(-N // B)
NP = NB * B
LASTP = (N - (NB - 1) * B) // G
ED = G * D
T = -(-E // P)
EFULL = E // T
EREST = E - EFULL * T
K = 4
NG = T // K
TRASH = K * P
HC = NB * G // 2
U = 4
EPS = 1e-5
assert T % K == 0 and LASTP * G + (NB - 1) * B == N and (T - EREST) > 0


def build(nc, x, src, dst, edge_type, W0, b0, W1, b1, W2, b2, W3, b3, gam3, bet3, Wr, Wl, bl, gam4, bet4, out):
    ctx = ExitStack()
    with ctx:
        def sb(name, shape, dt=F32):
            return ctx.enter_context(nc.sbuf_tensor(name, shape, dt))

        def sem(name):
            return ctx.enter_context(nc.semaphore(name))

        X = nc.dram_tensor("node_state", (NP, D), F32, kind="Internal").ap()
        Z = nc.dram_tensor("edge_sums", (NP + TRASH, D), F32, kind="Internal").ap()

        def batches(a, n):
            return a[0:n * B, :].rearrange("(b p g) f -> b p (g f)", p=P, g=G)

        Xb, Zb = batches(X, NB), batches(Z, NB)
        x_full, out_full = batches(x, NB - 1), batches(out, NB - 1)
        x_last = x[(NB - 1) * B:N, :].rearrange("(p g) f -> p (g f)", g=G)
        out_last = out[(NB - 1) * B:N, :].rearrange("(p g) f -> p (g f)", g=G)

        big = sb("big", [P, T * D])
        zin, xin, vv, xo, xT, zo = (big[:, i * U * ED:(i + 1) * U * ED].rearrange("p (s e) -> p s e", s=U)
                                    for i in range(6))
        messages = big[:, :].rearrange("p (g e) -> p g e", e=K * D)
        gat = sb("gathered_rows", [P, U, K * D])
        gatT = sb("gathered_rows_T", [P, 2, K * D])
        relmsg = sb("relation_messages", [P, 2, K * D])
        same = sb("same_target", [P, 2, K, K * P])
        sca = gat
        gidx = sb("gather_index_slot", [P, U, K], I32)
        sidx = sb("scatter_index_slot", [P, U, K], I32)
        kslot = sb("key_slot", [P, U, K])

        W0n, Wln = sb("W0_natural", [P, D]), sb("Wl_natural", [P, D])
        W0s, W1s, W2s, W3s, Wls = (sb(f"weight_{n}", [P, D]) for n in ("0", "1", "2", "3", "l"))
        Wrs = sb("weight_relations", [P, R * D])
        b0B, b2B, blB, g4B, e4B = (sb(f"row_{n}", [P, D]) for n in ("b0", "b2", "bl", "gam4", "bet4"))
        b1C, b3C, g3C, e3C = (sb(f"col_{n}", [P, 1]) for n in ("b1", "b3", "gam3", "bet3"))
        bnA, bnB = sb("bn_scale", [P, 1]), sb("bn_shift", [P, 1])
        ident = sb("ident", [P, P])
        eps = sb("eps", [P, 1])
        raw = sb("edges_raw", [P, 3, T], I32)
        key = sb("edges_key", [P, 2, T])
        eidx = sb("edges_index", [P, 2, T], I32)
        row = sb("edges_row", [P, 2, T])
        col = sb("edges_col", [P, 2, T])
        tmpi = sb("tmp_int", [P, 2, 2, T], I32)
        later = sb("later_same_target", [P, 2, T])
        latg = sb("later_slot", [P, U, K])
        sidxt = sb("scatter_index", [P, 2, T], I32)
        trash_i = sb("trash_int", [P, T], I32)
        trash = sb("trash", [P, T])
        typm = sb("type_mask", [P, R, T])
        after = sb("after_mask", [P, K, K * P])
        scr = sb("scratch", [P, K * P])
        ci = sb("column_int", [P, 2 * HC], I32)
        ch = sb("column_half", [P, 2 * HC], F16)
        ohp = sb("onehot_row", [P, U, P], F16)
        ohc = sb("onehot_col", [P, U, 2 * HC], F16)
        cS, cD = sb("rsqrt_deg_src", [P, 2 * HC]), sb("rsqrt_deg_dst", [P, 2 * HC])
        dg3, rd3 = sb("deg_in", [P, 2 * HC]), sb("recip_deg_in", [P, 2 * HC])
        st = sb("bn_six", [P, U, G, 6])
        mean2, diff, m2, var = (sb(n, [P, U, G]) for n in ("mean_twice", "mean_diff", "m2", "var128"))
        sd, rs, mean = (sb(n, [P, U, G]) for n in ("stddev", "rstd", "mean"))
        meanb, nshift = sb("mean_b", [P, U, G]), sb("neg_mean_rstd", [P, U, G])
        bns = sb("bn_stats_all", [P, 2 * (NB - 1) + G, 6])
        bnm = sb("bn_mean_var", [P, 2])
        bnt = sb("bn_tmp", [P, 4])

        ps = ctx.enter_context(nc.psum_tensor("ps", [P, 8, 512], F32))

        def pair(i):
            return ps[:, 2 * i:2 * i + 2, :].rearrange("p a (h f) -> p (a h) f", f=D)

        def pair_flat(i):
            return ps[:, 2 * i:2 * i + 2, :].rearrange("p a e -> p (a e)")

        def g3(a):
            return a.rearrange("p (g f) -> p g f", g=G)

        def per_node(table, b):
            return table[:, bass.ds(b * G, G)].unsqueeze(2).to_broadcast([P, G, D])

        def per_feature(r):
            return r[:, :].unsqueeze(1).to_broadcast([P, G, D])

        def known(v):
            return isinstance(v, int)

        def wait(eng, s, v):
            if not known(v) or v > 0:
                eng.wait_ge(s, v)

        def steps(eng, n, skew, body):
            head = min(n, U * -(-(skew + U) // U))
            rounds = (n - head) // U
            for t in range(head):
                body(t, t % U, lambda b: 0 <= b < n)
            if rounds:
                with eng.Fori(0, rounds) as i:
                    for u in range(U):
                        body(i * U + (head + u), u, lambda b: True)
            for t in range(head + rounds * U, n + skew):
                body(t, t % U, lambda b: 0 <= b < n)

        def nth(j, b, s, n=NB, unit=16):
            return j * -(-(n - s) // U) * unit + (b - s) * (unit // U) + unit

        def all_through(eng, ring, j, n=NB, unit=16):
            for s in range(U):
                eng.wait_ge(ring[s], (j + 1) * -(-(n - s) // U) * unit)

        def freed(eng, ring, j, b, s, n=NB, unit=16):
            if not known(b) or b >= U:
                eng.wait_ge(ring[s], nth(j, b - U, s, n, unit))

        def group(layer, b, s):
            return nth(layer, b, s, NG, 16 * K)

        def sems(name):
            return [sem(f"{name}_{s}") for s in range(U)]

        zin_in, xin_in, z_stored, x_stored = sems("zin_in"), sems("xin_in"), sems("z_stored"), sems("x_stored")
        raw_zero = sem("raw_zero")
        consts_in = sem("consts_in")
        N_CONST = 16 + 6
        pool_consts = sem("pool_consts")
        pchain = sem("pool_chain")
        keys_raw = sem("keys_raw")
        keys_padded = sem("keys_padded")
        prep = sem("vector_prep_chain")
        onehot = sem("onehot")
        hist_used = sem("hist_used")
        hist_done = sem("hist_done")
        deg1 = sem("deg_plus_one")
        deg_sqrt = sem("deg_sqrt")
        wT_ps, wT_sb = sem("weights_T_psum"), sem("weights_T_sbuf")
        keyrow, keyrow_used = sem("key_rows"), sem("key_rows_used")
        lat_in_slot, lat_chain = sem("later_in_slot"), sem("later_chain")
        prep_done = sem("prep_done")
        zeros_in = sem("trash_zeroed")
        prep_slot = sem("prep_key_slot")
        key_slot = sem("key_slot_in")
        begun = sem("indirect_group_begun")

        gidx_in = sem("gather_index_in")
        gathered = sems("gathered")
        keyR = sem("keyR")
        same_in = sem("same_in")
        grouped = sem("grouped")
        msg_in = sem("message_in")
        sca_in = sem("scatter_rows_in")
        sidx_in = sem("scatter_index_in")
        scattered = sem("scattered")
        gatT_ps, gatT_sb, rel_ps, rel_in, rel_chain = (sem(n) for n in (
            "gatheredT_psum", "gatheredT_sbuf", "relations_psum", "relation_msg_in", "relation_chain"))

        def node_pass(name, names, zl=0, xl=0, zs=0, xs=0):
            return dict(zl=zl, xl=xl, zs=zs, xs=xs, **{n: sem(f"{name}_{n}") for n in names.split()})

        p0 = node_pass("p0", "x_T xT_in proj biased z_out", xl=0, zs=0)
        p1 = node_pass("p1", "v ua dva var sd dvb x_out x_T xT_in proj z_out", zl=0, xl=1, zs=1, xs=0)
        p2 = node_pass("p2", "v x_T xT_in proj z_out", zl=1, zs=2)
        p3 = node_pass("p3", "v ua dva var sd dvb x_out x_T xT_in proj z_out", zl=2, xl=2, zs=3, xs=1)
        p4 = node_pass("p4", "v x_T stats", zl=3)
        p5 = node_pass("p5", "v v_T hT leaky h_back ua dva var sd dvb x_out x_T xT_in proj biased z_out",
                  zl=4, xl=3, zs=4, xs=2)
        p6 = node_pass("p6", "v xb dva var sd dvb dvc var2 sd2 fin o_out", zl=5, xl=4, xs=3)
        bn_chain, bn_sd, bn_ready = sem("bn_chain"), sem("bn_sd"), sem("bn_ready")

        block = ctx.enter_context(nc.Block())

        def after_p0(e):
            all_through(e, z_stored, p0["zs"])

        def after_edges(e, layer):
            e.wait_ge(scattered, 16 * T * (layer + 1))

        def after_p1(e):
            all_through(e, z_stored, p1["zs"])
            all_through(e, x_stored, p1["xs"])

        def after_p2(e):
            all_through(e, z_stored, p2["zs"])

        def after_p3(e):
            all_through(e, z_stored, p3["zs"])
            all_through(e, x_stored, p3["xs"])

        def after_p5(e):
            all_through(e, z_stored, p5["zs"])
            all_through(e, x_stored, p5["xs"])

        @block.sync
        def _(sp):
            for a, s in ((W0n, W0), (Wln, Wl), (W1s, W1), (W2s, W2), (W3s, W3)):
                sp.dma_start(a[:, :], s[:, :]).then_inc(consts_in, 16)
            sp.dma_start(Wrs[:, :].rearrange("i (r o) -> i r o", r=R),
                         Wr.rearrange("r i o -> i r o")).then_inc(consts_in, 16)
            for a, s in ((b0B, b0), (b2B, b2), (blB, bl), (g4B, gam4), (e4B, bet4)):
                sp.dma_start(a[:, :], s.unsqueeze(0).to_broadcast([P, D])).then_inc(consts_in, 16)
            for a, s in ((b1C, b1), (b3C, b3), (g3C, gam3), (e3C, bet3)):
                sp.dma_start(a[:, :], s.rearrange("(p o) -> p o", o=1)).then_inc(consts_in, 16)
            sp.wait_ge(raw_zero, 1)
            for i, s in enumerate((src, dst, edge_type)):
                sp.dma_start(raw[0:EFULL, i, :], s[0:EFULL * T].rearrange("(p t) -> p t", t=T)).then_inc(consts_in, 16)
                sp.dma_start(raw[EFULL:EFULL + 1, i, 0:EREST], s[EFULL * T:E].unsqueeze(0)).then_inc(consts_in, 16)
            sp.dma_start(Z[NP:NP + TRASH, :].rearrange("(p k) f -> p (k f)", k=K), scr[:, :]).then_inc(zeros_in, 16)

            def load_x(b, s, free, from_input):
                wait(sp, free, b - U + 1)
                if from_input and known(b) and b == NB - 1:
                    sp.dma_start(xin[0:LASTP, s, :], x_last).then_inc(xin_in[s], 16)
                else:
                    sp.dma_start(xin[:, s, :], (x_full if from_input else Xb)[b]).then_inc(xin_in[s], 16)

            def load_z(b, s, free):
                wait(sp, free, b - U + 1)
                sp.dma_start(zin[:, s, :], Zb[b]).then_inc(zin_in[s], 16)

            def load_steps(body):
                steps(sp, NB, 1, lambda t, s, live: body(t - 1, (s - 1) % U) if live(t - 1) else None)

            sp.wait_ge(prep_done, 1)
            load_steps(lambda b, s: load_x(b, s, p0["x_T"], True))
            after_edges(sp, 0)

            def p1_loads(b, s):
                load_z(b, s, p1["v"])
                load_x(b, s, p1["var"], True)
            load_steps(p1_loads)
            after_edges(sp, 1)
            load_steps(lambda b, s: load_z(b, s, p2["v"]))
            after_edges(sp, 2)

            def p3_loads(b, s):
                load_z(b, s, p3["v"])
                load_x(b, s, p3["var"], False)
            load_steps(p3_loads)
            after_edges(sp, 3)
            load_steps(lambda b, s: load_z(b, s, p4["v"]))
            sp.wait_ge(bn_ready, 1)

            def p5_loads(b, s):
                load_z(b, s, p5["h_back"])
                load_x(b, s, p5["var"], False)
            load_steps(p5_loads)
            after_edges(sp, 4)

            def p6_loads(b, s):
                load_z(b, s, p6["v"])
                load_x(b, s, p6["var2"], False)
            load_steps(p6_loads)
            sp.wait_ge(zeros_in, 16)
            all_through(sp, x_stored, p6["xs"])

        @block.gpsimd
        def _(pool):
            n = [0]

            def link(ins):
                n[0] += 1
                ins.then_inc(pchain, 1)
                pool.wait_ge(pchain, n[0])

            link(nc.gpsimd.memset(ident[:, :], 0.0))
            link(nc.gpsimd.affine_select(out=ident[:, :], in_=ident[:, :], compare_op=ALU.not_equal, fill=1.0, base=0,
                                         pattern=[[-1, P]], channel_multiplier=1))
            link(nc.gpsimd.memset(after[:, :, :], 1.0))
            for k in range(K):
                link(nc.gpsimd.affine_select(out=after[:, k, :], in_=after[:, k, :], compare_op=ALU.is_gt, fill=0.0,
                                             base=-k * P, pattern=[[1, K * P]], channel_multiplier=-1))
            nc.gpsimd.iota(trash_i[:, :], pattern=[[0, NG], [P, K]], base=NP, channel_multiplier=1)
            nc.gpsimd.iota(ci[:, :], pattern=[[1, 2 * HC]], base=0, channel_multiplier=0).then_inc(pool_consts, 1)
            pool.wait_ge(keys_raw, 1)
            for i in range(2):
                last = nc.gpsimd.affine_select(out=key[:, i, :], in_=key[:, i, :], compare_op=ALU.is_ge,
                                               fill=float(N), base=E - 1, pattern=[[-1, T]], channel_multiplier=-T)
            last.then_inc(keys_padded, 1)

            def gather(layer, table, rows):
                def body(t, s, live):
                    base = layer * NG
                    wait(pool, gidx_in, base + t + 1)
                    wait(pool, grouped, base + t - U + 1)
                    pool.sem_inc(begun, 1)
                    for k in range(K):
                        nc.gpsimd.indirect_dma_start(
                            out=gat[:, s, k * D:(k + 1) * D], out_offset=None, in_=rows,
                            in_offset=bass.IndirectOffsetOnAxis(ap=gidx[:, s, k:k + 1], axis=0)).then_inc(gathered[s], 16)
                steps(pool, NG, 0, body)

            def scatter(layer):
                all_through(pool, gathered, layer, NG, 16 * K)
                if layer == 0:
                    pool.wait_ge(zeros_in, 16)

                def body(t, s, live):
                    base = layer * NG
                    wait(pool, sca_in, base + t + 1)
                    wait(pool, sidx_in, base + t + 1)
                    wait(pool, scattered, (base + t) * 16 * K)
                    pool.sem_inc(begun, 1)
                    for k in range(K):
                        nc.gpsimd.indirect_dma_start(
                            out=Z[:, :], out_offset=bass.IndirectOffsetOnAxis(ap=sidx[:, s, k:k + 1], axis=0),
                            in_=sca[:, s, k * D:(k + 1) * D], in_offset=None,
                            compute_op=ALU.add).then_inc(scattered, 16)
                steps(pool, NG, 0, body)

            def scale(q, b, s, table, free):
                pool.wait_ge(zin_in[s], nth(q["zl"], b, s))
                wait(pool, free, b - U + 1)
                nc.gpsimd.tensor_tensor(g3(vv[:, s, :]), g3(zin[:, s, :]), per_node(table, b),
                                        ALU.mult).then_inc(q["v"], 1)

            def scale_out(q, b, s, table):
                pool.wait_ge(q["biased"], b + 1)
                nc.gpsimd.tensor_tensor(g3(zo[:, s, :]), g3(zo[:, s, :]), per_node(table, b),
                                        ALU.mult).then_inc(q["z_out"], 1)

            pool.wait_ge(prep_done, 1)
            steps(pool, NB, 0, lambda t, s, live: scale_out(p0, t, s, cS))
            after_p0(pool)
            gather(0, 1, Z[:, :])
            scatter(0)
            steps(pool, NB, 0, lambda t, s, live: scale(p1, t, s, cS, p1["x_out"]))
            after_p1(pool)
            gather(1, 0, Z[:, :])
            scatter(1)
            steps(pool, NB, 0, lambda t, s, live: scale(p2, t, s, cD, p2["x_T"]))
            after_p2(pool)
            gather(2, 0, Z[:, :])
            scatter(2)
            steps(pool, NB, 0, lambda t, s, live: scale(p3, t, s, cD, p3["x_out"]))
            after_p3(pool)
            gather(3, 0, Z[:, :])
            scatter(3)
            steps(pool, NB, 0, lambda t, s, live: scale(p4, t, s, cD, p4["x_T"]))

            def p5_body(t, s, live):
                if live(t - 6):
                    scale_out(p5, t - 6, (s - 6) % U, dg3)
                if live(t):
                    scale(p5, t, s, cD, p5["x_out"])
            steps(pool, NB, 6, p5_body)
            after_p5(pool)
            gather(4, 0, X[:, :])
            scatter(4)

            def p6_body(t, s, live):
                scale(p6, t, s, rd3, p6["o_out"])
                pool.wait_ge(xin_in[s], nth(p6["xl"], t, s))
                nc.gpsimd.tensor_tensor(g3(xin[:, s, :]), g3(xin[:, s, :]), per_feature(e4B),
                                        ALU.add).then_inc(p6["xb"], 1)
            steps(pool, NB, 0, p6_body)

        @block.scalar
        def _(act):
            act.wait_ge(wT_ps, 1)
            nc.scalar.activation(W0s[:, :], ps[:, 6, 0:D], ACT.Copy)
            nc.scalar.activation(Wls[:, :], ps[:, 6, D:2 * D], ACT.Copy).then_inc(wT_sb, 1)
            act.wait_ge(deg1, 1)
            nc.scalar.activation(cS[:, :], cS[:, :], ACT.Sqrt)
            nc.scalar.activation(cD[:, :], cD[:, :], ACT.Sqrt).then_inc(deg_sqrt, 1)

            act.wait_ge(keys_padded, 1)
            for i in range(2):
                wait(act, keyrow, i * NG)
                def stage_keys(t, s, live):
                    wait(act, keyrow, i * NG + t - U + 1)
                    nc.scalar.activation(kslot[:, s, :], key[:, i, bass.ds(t * K, K)],
                                         ACT.Copy).then_inc(prep_slot, 1)
                steps(act, NG, 0, stage_keys)

            def evac(q, b, s, func, bias):
                act.wait_ge(q["x_T"], b + 1)
                wait(act, q["proj"], b - U + 1)
                if bias is None:
                    nc.scalar.activation(xT[:, s, :], pair_flat(s % 2 if q is not p5 else 2), func).then_inc(q["xT_in"], 1)
                else:
                    nc.scalar.activation(xT[:, s, :], pair_flat(s % 2), func, bias=bias).then_inc(q["xT_in"], 1)

            def root(q, b, s, var_sem, sd_sem, free):
                act.wait_ge(var_sem, b + 1)
                wait(act, free, b - U + 1)
                nc.scalar.activation(sd[:, s, :], var[:, s, :], ACT.Sqrt, bias=eps[:, 0:1],
                                     scale=1.0 / D).then_inc(sd_sem, 1)

            def project_out(q, b, s, table):
                act.wait_ge(q["proj"], b + 1)
                freed(act, z_stored, q["zs"], b, s)
                for g in range(G):
                    last = nc.scalar.activation(zo[:, s, g * D:(g + 1) * D], pair(2 + s % 2)[:, g, :], ACT.Copy,
                                                scale=table[:, bass.ds(b * G + g, 1)])
                last.then_inc(q["z_out"], 1)

            def store_z(q, b, s):
                act.wait_ge(q["z_out"], b + 1)
                act.dma_start(Zb[b], zo[:, s, :]).then_inc(z_stored[s], 16)

            def store_x(q, b, s):
                act.wait_ge(q["x_out"], b + 1)
                act.dma_start(Xb[b], xo[:, s, :]).then_inc(x_stored[s], 16)

            def edges(layer):
                base = layer * NG

                def body(t, s, live):
                    if live(t - 1):
                        b = t - 1
                        act.wait_ge(grouped, base + b + 1)
                        nc.scalar.activation(messages[:, bass.ds(b, 1), :].rearrange("p a e -> p (a e)"),
                                             ps[:, 2 + (s - 1) % 2 if layer < 4 else 2, :], ACT.Copy).then_inc(msg_in, 1)
                    if layer == 4 and live(t):
                        act.wait_ge(gatT_ps, t + 1)
                        wait(act, rel_ps, t - 2 + 1)
                        nc.scalar.activation(gatT[:, s % 2, :], ps[:, 3, :], ACT.Copy).then_inc(gatT_sb, 1)
                steps(act, NG, 1, body)

                def copies(t, s, live):
                    act.wait_ge(msg_in, base + NG) if known(t) and t == 0 else None
                    if known(t) and t == 0:
                        all_through(act, gathered, layer, NG, 16 * K)
                    wait(act, scattered, (base + t - U + 1) * 16 * K)
                    nc.scalar.activation(sca[:, s, :], messages[:, bass.ds(t, 1), :].rearrange("p a e -> p (a e)"),
                                         ACT.Copy).then_inc(sca_in, 1)
                steps(act, NG, 0, copies)

            def p0_body(t, s, live):
                if live(t - 3):
                    store_z(p0, t - 3, (s - 3) % U)
                if live(t):
                    evac(p0, t, s, ACT.Copy, None)
            act.wait_ge(prep_done, 1)
            steps(act, NB, 3, p0_body)
            after_p0(act)
            edges(0)

            def mid(q, table):
                def body(t, s, live):
                    if live(t - 3):
                        project_out(q, t - 3, (s - 3) % U, table)
                        store_z(q, t - 3, (s - 3) % U)
                    if live(t - 2):
                        evac(q, t - 2, (s - 2) % U, ACT.Copy, None)
                        store_x(q, t - 2, (s - 2) % U)
                    if live(t):
                        root(q, t, s, q["var"], q["sd"], q["x_out"])
                steps(act, NB, 3, body)
            after_edges(act, 0)
            mid(p1, cD)
            after_p1(act)
            edges(1)
            after_edges(act, 1)

            def p2_body(t, s, live):
                if live(t - 1):
                    project_out(p2, t - 1, (s - 1) % U, cD)
                    store_z(p2, t - 1, (s - 1) % U)
                if live(t):
                    evac(p2, t, s, ACT.Relu, b1C[:, 0:1])
            steps(act, NB, 1, p2_body)
            after_p2(act)
            edges(2)
            after_edges(act, 2)
            mid(p3, cS)
            after_p3(act)
            edges(3)
            act.wait_ge(bn_chain, 1)
            nc.scalar.activation(bnt[:, 0:1], bnm[:, 1:2], ACT.Sqrt, bias=eps[:, 0:1]).then_inc(bn_sd, 1)
            act.wait_ge(bn_ready, 1)

            def p5_body(t, s, live):
                if live(t - 6):
                    store_z(p5, t - 6, (s - 6) % U)
                if live(t - 4):
                    evac(p5, t - 4, (s - 4) % U, ACT.Copy, None)
                    store_x(p5, t - 4, (s - 4) % U)
                if live(t - 2):
                    root(p5, t - 2, (s - 2) % U, p5["var"], p5["sd"], p5["x_out"])
                if live(t):
                    act.wait_ge(p5["v_T"], t + 1)
                    wait(act, p5["h_back"], t - U + 1)
                    nc.scalar.activation(zin[:, s, :], pair_flat(0), ACT.Identity, bias=bnB[:, 0:1],
                                         scale=bnA[:, 0:1]).then_inc(p5["hT"], 1)
            steps(act, NB, 6, p5_body)
            after_p5(act)
            edges(4)
            after_edges(act, 4)

            def p6_body(t, s, live):
                b, q = t - 3, (s - 3) % U
                if live(b):
                    act.wait_ge(p6["fin"], b + 1)
                    freed(act, x_stored, p6["xs"], b, q)
                    for g in range(G):
                        last = nc.scalar.activation(xo[:, q, g * D:(g + 1) * D], vv[:, q, g * D:(g + 1) * D],
                                                    ACT.Identity, bias=nshift[:, q, g:g + 1], scale=rs[:, q, g:g + 1])
                    last.then_inc(p6["o_out"], 1)
                    act.wait_ge(p6["o_out"], b + 1)
                    if known(b) and b == NB - 1:
                        act.dma_start(out_last, xo[0:LASTP, q, :]).then_inc(x_stored[q], 16)
                    else:
                        act.dma_start(out_full[b], xo[:, q, :]).then_inc(x_stored[q], 16)
                if live(t - 1):
                    act.wait_ge(p6["var2"], t)
                    wait(act, p6["fin"], t - 1 - U + 1)
                    nc.scalar.activation(mean2_sd(s - 1), var[:, (s - 1) % U, :], ACT.Sqrt, bias=eps[:, 0:1],
                                         scale=1.0 / D).then_inc(p6["sd2"], 1)
                if live(t):
                    root(p6, t, s, p6["var"], p6["sd"], p6["var2"])

            def mean2_sd(s):
                return m2[:, s % U, :]
            steps(act, NB, 3, p6_body)

        @block.vector
        def _(dve):
            n = [0]

            def link(ins):
                n[0] += 1
                ins.then_inc(prep, 1)
                dve.wait_ge(prep, n[0])

            nc.vector.memset(raw[:, :, :], 0)
            nc.vector.memset(eps[:, :], EPS)
            nc.vector.memset(scr[:, :], 0.0).then_inc(raw_zero, 1)
            dve.wait_ge(consts_in, 16 * (15 + 6))
            nc.vector.tensor_copy(key[:, :, :], raw[:, 0:2, :]).then_inc(keys_raw, 1)
            for r in range(R):
                nc.vector.tensor_scalar(typm[:, r, :], raw[:, 2, :], float(r), None, ALU.is_equal)
            dve.wait_ge(pool_consts, 1)
            nc.vector.tensor_copy(trash[:, :], trash_i[:, :])
            nc.vector.tensor_copy(ch[:, :], ci[:, :])
            dve.wait_ge(keys_padded, 1)
            link(nc.vector.tensor_copy(eidx[:, :, :], key[:, :, :]))
            nc.vector.tensor_scalar(tmpi[:, 0, :, :], eidx[:, :, :], 3, P - 1, ALU.logical_shift_right,
                                    ALU.bitwise_and)
            nc.vector.tensor_scalar(tmpi[:, 1, :, :], eidx[:, :, :], 10, 3, ALU.logical_shift_right,
                                    ALU.logical_shift_left)
            link(nc.vector.tensor_copy(later[:, :, :], key[:, :, :]))
            link(nc.vector.tensor_copy(row[:, :, :], tmpi[:, 0, :, :]))
            link(nc.vector.tensor_copy(col[:, :, :], tmpi[:, 1, :, :]))
            link(nc.vector.tensor_scalar(tmpi[:, 0, :, :], eidx[:, :, :], G - 1, None, ALU.bitwise_and))
            link(nc.vector.tensor_copy(later[:, :, :], tmpi[:, 0, :, :]))
            link(nc.vector.tensor_tensor(col[:, :, :], col[:, :, :], later[:, :, :], ALU.add))

            for i in range(2):
                def body(t, s, live):
                    wait(dve, hist_used, i * T + t - U + 1)
                    nc.vector.tensor_scalar(ohp[:, s, :], ch[:, 0:P], row[:, i, bass.ds(t, 1)], None, ALU.is_equal)
                    nc.vector.tensor_scalar(ohc[:, s, :], ch[:, :], col[:, i, bass.ds(t, 1)], None,
                                            ALU.is_equal).then_inc(onehot, 1)
                steps(dve, T, 0, body)

            def hist(i):
                return ps[:, 2 * i:2 * i + 2, 0:HC]

            def halves(a):
                return a[:, :].rearrange("p (a c) -> p a c", a=2)

            dve.wait_ge(hist_done, 2)
            nc.vector.tensor_scalar(halves(cS), hist(0), 1.0, None, ALU.add)
            link(nc.vector.tensor_scalar(halves(dg3), hist(1), 1.0, None, ALU.max))
            nc.vector.reciprocal(rd3[:, :], dg3[:, :])
            nc.vector.tensor_scalar(halves(cD), hist(1), 1.0, None, ALU.add).then_inc(deg1, 1)
            dve.wait_ge(deg_sqrt, 1)
            nc.vector.reciprocal(cS[:, :], cS[:, :])
            link(nc.vector.reciprocal(cD[:, :], cD[:, :]))

            dve.wait_ge(zeros_in, 16)
            for i in range(2):
                wait(dve, keyrow_used, i * NG)
                def body(t, s, live):
                    m = i * NG + t
                    dve.wait_ge(keyrow, m + 1)
                    for k in range(K):
                        last = nc.vector.scalar_tensor_tensor(
                            out=scr[:, :], in0=ps[:, 4 + s % 2, :], scalar=key[:, i, bass.ds(t * K + k, 1)],
                            in1=after[:, k, :], op0=ALU.is_equal, op1=ALU.mult, accum_out=latg[:, s, k:k + 1])
                        last.then_inc(lat_chain, 1)
                        dve.wait_ge(lat_chain, m * K + (k + 1))
                    nc.vector.tensor_copy(later[:, i, bass.ds(t * K, K)], latg[:, s, :]).then_inc(keyrow_used, 1)
                steps(dve, NG, 0, body)
            dve.wait_ge(keyrow_used, 2 * NG)
            link(nc.vector.tensor_scalar(later[:, :, :], later[:, :, :], 1.0, None, ALU.min))
            for i in range(2):
                link(nc.vector.tensor_tensor(row[:, i, :], trash[:, :], key[:, i, :], ALU.subtract))
            link(nc.vector.tensor_tensor(row[:, :, :], row[:, :, :], later[:, :, :], ALU.mult))
            link(nc.vector.tensor_tensor(row[:, :, :], row[:, :, :], key[:, :, :], ALU.add))
            dve.wait_ge(wT_sb, 1)
            nc.vector.tensor_copy(sidxt[:, :, :], row[:, :, :]).then_inc(prep_done, 1)

            def edges(layer, gi, ki):
                base = layer * NG

                def body(t, s, live):
                    if live(t - 1):
                        b, q = t - 1, (s - 1) % U
                        dve.wait_ge(keyR, base + b + 1)
                        wait(dve, grouped, base + b - 2 + 1)
                        for k in range(K):
                            last = nc.vector.tensor_scalar(same[:, q % 2, k, :], ps[:, q % 2, :],
                                                           key[:, ki, bass.ds(b * K + k, 1)], None, ALU.is_equal)
                        last.then_inc(same_in, 1)
                        if layer == 4:
                            dve.wait_ge(rel_ps, b + 1)
                            wait(dve, grouped, base + b - 2 + 1)
                            for k in range(K):
                                m = relmsg[:, q % 2, k * D:(k + 1) * D]
                                nc.vector.tensor_scalar(m, ps[:, 4 + k, 0:D], typm[:, 0, bass.ds(b * K + k, 1)],
                                                        None, ALU.mult).then_inc(rel_chain, 1)
                            for r in range(1, R):
                                for k in range(K):
                                    m = relmsg[:, q % 2, k * D:(k + 1) * D]
                                    if k == 0:
                                        dve.wait_ge(rel_chain, b * K * R + r * K)
                                    nc.vector.scalar_tensor_tensor(
                                        out=m, in0=ps[:, 4 + k, r * D:(r + 1) * D],
                                        scalar=typm[:, r, bass.ds(b * K + k, 1)], in1=m, op0=ALU.mult,
                                        op1=ALU.add).then_inc(rel_chain, 1)
                    if live(t):
                        freed(dve, gathered, layer, t, s, NG, 16 * K)
                        nc.vector.tensor_copy(gidx[:, s, :], eidx[:, gi, bass.ds(t * K, K)]).then_inc(gidx_in, 1)
                        wait(dve, keyR, base + t - U + 1)
                        nc.vector.tensor_copy(kslot[:, s, :], key[:, ki, bass.ds(t * K, K)]).then_inc(key_slot, 1)
                steps(dve, NG, 1, body)

                def indices(t, s, live):
                    wait(dve, scattered, (base + t - U + 1) * 16 * K)
                    nc.vector.tensor_copy(sidx[:, s, :], sidxt[:, ki, bass.ds(t * K, K)]).then_inc(sidx_in, 1)
                steps(dve, NG, 0, indices)

            def ln_stats(a, b, s, chain, per, j, done):
                for g in range(G):
                    last = nc.vector.bn_stats(st[:, s, g, :], a[:, g, :])
                last.then_inc(chain, 1)
                dve.wait_ge(chain, b * per + (j + 1))
                nc.vector.tensor_tensor(diff[:, s, :], st[:, s, :, 1], st[:, s, :, 4], ALU.subtract)
                nc.vector.tensor_tensor(mean2[:, s, :], st[:, s, :, 1], st[:, s, :, 4], ALU.add)
                nc.vector.tensor_tensor(var[:, s, :], st[:, s, :, 2], st[:, s, :, 5], ALU.add).then_inc(chain, 1)
                dve.wait_ge(chain, b * per + (j + 2))
                nc.vector.tensor_scalar(mean[:, s, :], mean2[:, s, :], 0.5, None, ALU.mult)
                nc.vector.tensor_tensor(diff[:, s, :], diff[:, s, :], diff[:, s, :], ALU.mult).then_inc(chain, 1)
                dve.wait_ge(chain, b * per + (j + 3))
                nc.vector.scalar_tensor_tensor(out=var[:, s, :], in0=diff[:, s, :], scalar=D / 4.0, in1=var[:, s, :],
                                               op0=ALU.mult, op1=ALU.add).then_inc(done, 1)

            def ln_apply(out_, a, s, means, scales):
                for g in range(G):
                    last = nc.vector.tensor_scalar(out_[:, g, :], a[:, g, :], means[:, s, g:g + 1],
                                                   scales[:, s, g:g + 1], ALU.subtract, ALU.mult)
                return last

            def norm_out(q, b, s):
                dve.wait_ge(q["sd"], b + 1)
                nc.vector.reciprocal(rs[:, s, :], sd[:, s, :]).then_inc(q["dvb"], 1)
                wait(dve, q["x_T"], b - U + 1)
                freed(dve, x_stored, q["xs"], b, s)
                dve.wait_ge(q["dvb"], b + 1)
                ln_apply(g3(xo[:, s, :]), g3(vv[:, s, :]), s, mean, rs).then_inc(q["x_out"], 1)

            def biased(q, b, s, bias, bank):
                dve.wait_ge(q["proj"], b + 1)
                freed(dve, z_stored, q["zs"], b, s)
                nc.vector.tensor_tensor(g3(zo[:, s, :]), pair(bank), per_feature(bias), ALU.add).then_inc(q["biased"], 1)

            steps(dve, NB, 0, lambda t, s, live: biased(p0, t, s, b0B, 2 + s % 2))
            after_p0(dve)
            edges(0, 1, 0)
            after_edges(dve, 0)

            def p1_body(t, s, live):
                if live(t - 1):
                    norm_out(p1, t - 1, (s - 1) % U)
                if live(t):
                    dve.wait_ge(p1["v"], t + 1)
                    dve.wait_ge(xin_in[s], nth(p1["xl"], t, s))
                    nc.vector.scalar_tensor_tensor(out=vv[:, s, :], in0=vv[:, s, :], scalar=0.0, in1=xin[:, s, :],
                                                   op0=ALU.max, op1=ALU.add).then_inc(p1["ua"], 1)
                    dve.wait_ge(p1["ua"], t + 1)
                    ln_stats(g3(vv[:, s, :]), t, s, p1["dva"], 3, 0, p1["var"])
            steps(dve, NB, 1, p1_body)
            after_p1(dve)
            edges(1, 0, 1)
            after_p2(dve)
            edges(2, 0, 1)
            after_edges(dve, 2)

            def p3_body(t, s, live):
                if live(t - 1):
                    norm_out(p3, t - 1, (s - 1) % U)
                if live(t):
                    dve.wait_ge(p3["v"], t + 1)
                    nc.vector.tensor_tensor(g3(vv[:, s, :]), g3(vv[:, s, :]), per_feature(b2B),
                                            ALU.add).then_inc(p3["ua"], 1)
                    dve.wait_ge(p3["ua"], 2 * t + 1)
                    dve.wait_ge(xin_in[s], nth(p3["xl"], t, s))
                    nc.vector.tensor_tensor(vv[:, s, :], vv[:, s, :], xin[:, s, :], ALU.add).then_inc(p3["ua"], 1)
                    dve.wait_ge(p3["ua"], 2 * t + 2)
                    ln_stats(g3(vv[:, s, :]), t, s, p3["dva"], 3, 0, p3["var"])
            steps(dve, NB, 1, p3_body)
            after_p3(dve)
            edges(3, 0, 1)
            after_edges(dve, 3)

            def p4_body(t, s, live):
                dve.wait_ge(p4["x_T"], t + 1)
                if known(t) and t == NB - 1:
                    for g in range(G):
                        last = nc.vector.bn_stats(bns[:, 2 * (NB - 1) + g, :], pair(s)[:, g, 0:LASTP])
                else:
                    for h in range(2):
                        last = nc.vector.bn_stats(bns[:, bass.ds(t * 2 + h, 1), :].rearrange("p a e -> p (a e)"),
                                                  ps[:, 2 * s + h, :])
                last.then_inc(p4["stats"], 1)
            steps(dve, NB - 1, 0, p4_body)
            p4_body(NB - 1, (NB - 1) % U, None)
            dve.wait_ge(p4["stats"], NB)
            nc.vector.bn_aggr(bnm[:, :], bns[:, :, :].rearrange("p a e -> p (a e)")).then_inc(bn_chain, 1)
            dve.wait_ge(bn_chain, 1)
            nc.vector.tensor_tensor(bnt[:, 1:2], bnm[:, 0:1], b3C[:, :], ALU.add).then_inc(bn_chain, 1)
            dve.wait_ge(bn_sd, 1)
            nc.vector.reciprocal(bnt[:, 2:3], bnt[:, 0:1]).then_inc(bn_chain, 1)
            dve.wait_ge(bn_chain, 3)
            nc.vector.tensor_tensor(bnA[:, :], bnt[:, 2:3], g3C[:, :], ALU.mult).then_inc(bn_chain, 1)
            nc.vector.tensor_tensor(bnt[:, 3:4], b3C[:, :], bnt[:, 1:2], ALU.subtract).then_inc(bn_chain, 1)
            dve.wait_ge(bn_chain, 5)
            nc.vector.tensor_tensor(bnB[:, :], bnt[:, 3:4], bnA[:, :], ALU.mult).then_inc(bn_chain, 1)
            dve.wait_ge(bn_chain, 6)
            nc.vector.tensor_tensor(bnB[:, :], bnB[:, :], e3C[:, :], ALU.add).then_inc(bn_ready, 1)

            def p5_body(t, s, live):
                if live(t - 5):
                    biased(p5, t - 5, (s - 5) % U, blB, 3)
                if live(t - 2):
                    norm_out(p5, t - 2, (s - 2) % U)
                if live(t - 1):
                    b, q = t - 1, (s - 1) % U
                    dve.wait_ge(p5["h_back"], b + 1)
                    dve.wait_ge(xin_in[q], nth(p5["xl"], b, q))
                    nc.vector.tensor_tensor(g3(vv[:, q, :]), pair(1), g3(xin[:, q, :]), ALU.add).then_inc(p5["ua"], 1)
                    dve.wait_ge(p5["ua"], b + 1)
                    ln_stats(g3(vv[:, q, :]), b, q, p5["dva"], 3, 0, p5["var"])
                if live(t):
                    dve.wait_ge(p5["hT"], t + 1)
                    nc.vector.scalar_tensor_tensor(out=zin[:, s, :], in0=zin[:, s, :], scalar=0.01, in1=zin[:, s, :],
                                                   op0=ALU.mult, op1=ALU.max).then_inc(p5["leaky"], 1)
            steps(dve, NB, 5, p5_body)
            after_p5(dve)
            edges(4, 0, 1)
            after_edges(dve, 4)

            def p6_body(t, s, live):
                if live(t - 2):
                    b, q = t - 2, (s - 2) % U
                    dve.wait_ge(p6["sd2"], b + 1)
                    nc.vector.reciprocal(rs[:, q, :], m2[:, q, :]).then_inc(p6["dvc"], 1)
                    dve.wait_ge(p6["dvc"], b + 1)
                    nc.vector.scalar_tensor_tensor(out=nshift[:, q, :], in0=mean[:, q, :], scalar=-1.0,
                                                   in1=rs[:, q, :], op0=ALU.mult, op1=ALU.mult).then_inc(p6["fin"], 1)
                if live(t - 1):
                    b, q = t - 1, (s - 1) % U
                    v = vv[:, q, :]
                    dve.wait_ge(p6["sd"], b + 1)
                    nc.vector.reciprocal(rs[:, q, :], sd[:, q, :]).then_inc(p6["dvb"], 1)
                    dve.wait_ge(p6["dvb"], b * 7 + 1)
                    ln_apply(g3(v), g3(v), q, mean, rs).then_inc(p6["dvb"], 1)
                    dve.wait_ge(p6["dvb"], b * 7 + 2)
                    nc.vector.tensor_tensor(g3(v), g3(v), per_feature(g4B), ALU.mult).then_inc(p6["dvb"], 1)
                    dve.wait_ge(p6["dvb"], b * 7 + 3)
                    dve.wait_ge(p6["xb"], b + 1)
                    nc.vector.tensor_tensor(v, v, xin[:, q, :], ALU.add).then_inc(p6["dvb"], 1)
                    dve.wait_ge(p6["dvb"], b * 7 + 4)
                    ln_stats(g3(v), b, q, p6["dvb"], 7, 4, p6["var2"])
                if live(t):
                    dve.wait_ge(p6["v"], t + 1)
                    ln_stats(g3(vv[:, s, :]), t, s, p6["dva"], 3, 0, p6["var"])
            steps(dve, NB, 2, p6_body)

        @block.tensor
        def _(pe):
            pe.wait_ge(consts_in, 16 * (15 + 6))
            pe.wait_ge(pool_consts, 1)
            nc.tensor.transpose(ps[:, 6, 0:D], W0n[:, :], ident[:, :])
            nc.tensor.transpose(ps[:, 6, D:2 * D], Wln[:, :], ident[:, :]).then_inc(wT_ps, 1)

            for i in range(2):
                def count(t, s, first, final):
                    pe.wait_ge(onehot, i * T + t + 1)
                    for h in range(2):
                        last = nc.tensor.matmul(ps[:, 2 * i + h, 0:HC], ohp[:, s, :], ohc[:, s, h * HC:(h + 1) * HC],
                                                start=first, stop=final)
                    last.then_inc(hist_used, 1)
                    return last
                for t in range(U):
                    count(t, t, t == 0, False)
                with pe.Fori(0, T // U - 2) as j:
                    for u in range(U):
                        count(j * U + (U + u), u, False, False)
                for t in range(T - U, T):
                    count(t, t % U, False, t == T - 1)
                pe.wait_ge(hist_used, (i + 1) * T)
                pe.sem_inc(hist_done, 1)

            def key_rows(s, bank, done):
                for k in range(K):
                    last = nc.tensor.transpose(ps[:, bank, k * P:(k + 1) * P],
                                               kslot[:, s, k:k + 1].to_broadcast([P, P]), ident[:, :])
                last.then_inc(done, 1)

            for i in range(2):
                wait(pe, keyrow_used, i * NG)
                def body(t, s, live):
                    wait(pe, keyrow_used, i * NG + t - 2 + 1)
                    pe.wait_ge(prep_slot, i * NG + t + 1)
                    key_rows(s, 4 + s % 2, keyrow)
                steps(pe, NG, 0, body)
            pe.wait_ge(prep_done, 1)

            def transpose_batch(a, bank, done):
                for g in range(G):
                    last = nc.tensor.transpose(pair(bank)[:, g, :], a[:, g * D:(g + 1) * D], ident[:, :])
                last.then_inc(done, 1)

            def project(q, b, s, weight, bank, free, lag):
                pe.wait_ge(q["xT_in"], b + 1)
                wait(pe, free, b - lag + 1)
                for g in range(G):
                    last = nc.tensor.matmul(pair(bank)[:, g, :], xT[:, s, g * D:(g + 1) * D], weight[:, :],
                                            start=True, stop=True)
                last.then_inc(q["proj"], 1)

            def edges(layer, ki):
                base = layer * NG

                def body(t, s, live):
                    if live(t - 1):
                        b, q = t - 1, (s - 1) % U
                        pe.wait_ge(gathered[q], group(layer, b, q))
                        rows, bank = gat[:, q, :], 2 + q % 2
                        if layer == 4:
                            bank = 2
                            wait(pe, gatT_sb, b)
                            for k in range(K):
                                last = nc.tensor.transpose(ps[:, 3, k * P:(k + 1) * P], gat[:, q, k * D:(k + 1) * D],
                                                           ident[:, :])
                            last.then_inc(gatT_ps, 1)
                            pe.wait_ge(gatT_sb, b + 1)
                            wait(pe, rel_chain, b * K * R)
                            for k in range(K):
                                last = nc.tensor.matmul(ps[:, 4 + k, 0:R * D], gatT[:, q % 2, k * P:(k + 1) * P],
                                                        Wrs[:, :], start=True, stop=True)
                            last.then_inc(rel_ps, 1)
                            pe.wait_ge(rel_chain, (b + 1) * K * R)
                            rows = relmsg[:, q % 2, :]
                            wait(pe, msg_in, base + b)
                        else:
                            wait(pe, msg_in, base + b - 2 + 1)
                        pe.wait_ge(same_in, base + b + 1)
                        for j in range(K):
                            for k in range(K):
                                last = nc.tensor.matmul(ps[:, bank, j * D:(j + 1) * D],
                                                        same[:, q % 2, k, j * P:(j + 1) * P],
                                                        rows[:, k * D:(k + 1) * D], start=k == 0, stop=k == K - 1)
                        last.then_inc(grouped, 1)
                    if live(t):
                        wait(pe, same_in, base + t - 2 + 1)
                        pe.wait_ge(key_slot, base + t + 1)
                        key_rows(s, s % 2, keyR)
                steps(pe, NG, 1, body)

            def plain(q, a, weight, free):
                def body(t, s, live):
                    if live(t - 1):
                        project(q, t - 1, (s - 1) % U, weight, 2 + (s - 1) % 2, free, 2)
                    if live(t):
                        a(t, s)
                        wait(pe, q["xT_in"], t - 2 + 1)
                        transpose_batch(ring(q)[:, s, :], s % 2, q["x_T"])
                steps(pe, NB, 1, body)

            def ring(q):
                return xin if q is p0 else vv if q is p2 else xo

            plain(p0, lambda t, s: pe.wait_ge(xin_in[s], nth(p0["xl"], t, s)), W0s, p0["biased"])
            after_p0(pe)
            edges(0, 0)
            after_edges(pe, 0)
            plain(p1, lambda t, s: pe.wait_ge(p1["x_out"], t + 1), W1s, p1["z_out"])
            after_p1(pe)
            edges(1, 1)
            after_edges(pe, 1)
            plain(p2, lambda t, s: pe.wait_ge(p2["v"], t + 1), W2s, p2["z_out"])
            after_p2(pe)
            edges(2, 1)
            after_edges(pe, 2)
            plain(p3, lambda t, s: pe.wait_ge(p3["x_out"], t + 1), W3s, p3["z_out"])
            after_p3(pe)
            edges(3, 1)
            after_edges(pe, 3)

            def p4_body(t, s, live):
                pe.wait_ge(p4["v"], t + 1)
                wait(pe, p4["stats"], t - U + 1)
                transpose_batch(vv[:, s, :], s, p4["x_T"])
            steps(pe, NB, 0, p4_body)
            pe.wait_ge(bn_ready, 1)

            def p5_body(t, s, live):
                if live(t - 5):
                    project(p5, t - 5, (s - 5) % U, Wls, 3, p5["biased"], 1)
                if live(t - 4):
                    b, q = t - 4, (s - 4) % U
                    pe.wait_ge(p5["x_out"], b + 1)
                    wait(pe, p5["xT_in"], b)
                    transpose_batch(xo[:, q, :], 2, p5["x_T"])
                if live(t - 1):
                    b, q = t - 1, (s - 1) % U
                    pe.wait_ge(p5["leaky"], b + 1)
                    wait(pe, p5["ua"], b)
                    transpose_batch(zin[:, q, :], 1, p5["h_back"])
                if live(t):
                    pe.wait_ge(p5["v"], t + 1)
                    wait(pe, p5["hT"], t)
                    transpose_batch(vv[:, s, :], 0, p5["v_T"])
            steps(pe, NB, 5, p5_body)
            after_p5(pe)
            edges(4, 1)


_INS = ['x', 'src', 'dst', 'edge_type_3', 'L0_gnn_W', 'L0_gnn_b', 'L1_gnn_W1', 'L1_gnn_b1', 'L1_gnn_W2', 'L1_gnn_b2',
        'L2_gnn_W', 'L2_gnn_b', 'L2_gnn_gamma', 'L2_gnn_beta', 'L3_gnn_relation_weights', 'L3_gnn_lin_w',
        'L3_gnn_lin_b', 'L3_gnn_ln_gamma', 'L3_gnn_ln_beta']


def kernel(**inputs):
    import numpy as _np
    import concourse.bacc as _bacc
    from concourse import mybir as _mybir
    from concourse.bass_utils import run_bass_kernel_spmd as _run

    nc = _bacc.Bacc("TRN2", target_bir_lowering=False, num_devices=1)
    arrays, args = {}, []
    for name in _INS:
        a = _np.ascontiguousarray(inputs[name])
        arrays[f"in_{name}_dram"] = a
        args.append(nc.dram_tensor(f"in_{name}_dram", a.shape, _mybir.dt.from_np(a.dtype), kind="ExternalInput").ap())
    args.append(nc.dram_tensor("out_dram", (N, D), F32, kind="ExternalOutput").ap())
    build(nc, *args)
    r = _run(nc, [arrays], core_ids=[0])
    return r.results[0]["out_dram"]
```

```python
import numpy as np
import concourse.bass as bass
from concourse import mybir
from concourse.alu_op_type import AluOpType as ALU
from contextlib import ExitStack

F32 = mybir.dt.float32
F16 = mybir.dt.float16
I32 = mybir.dt.int32
ACT = mybir.ActivationFunctionType

P = 128
N = 100000
D = 128
E = 25000
R = 3
G = 8
B = P * G
NB = -(-N // B)
NP = NB * B
LASTP = (N - (NB - 1) * B) // G
ED = G * D
T = -(-E // P)
EFULL = E // T
EREST = E - EFULL * T
K = 4
NG = T // K
TRASH = K * P
HC = NB * G // 2
U = 4
EPS = 1e-5
assert T % K == 0 and LASTP * G + (NB - 1) * B == N and (T - EREST) > 0


def build(nc, x, src, dst, edge_type, W0, b0, W1, b1, W2, b2, W3, b3, gam3, bet3, Wr, Wl, bl, gam4, bet4, out):
    ctx = ExitStack()
    with ctx:
        def sb(name, shape, dt=F32):
            return ctx.enter_context(nc.sbuf_tensor(name, shape, dt))

        def sem(name):
            return ctx.enter_context(nc.semaphore(name))

        X = nc.dram_tensor("node_state", (NP, D), F32, kind="Internal").ap()
        Z = nc.dram_tensor("edge_sums", (NP + TRASH, D), F32, kind="Internal").ap()

        def batches(a, n):
            return a[0:n * B, :].rearrange("(b p g) f -> b p (g f)", p=P, g=G)

        Xb, Zb = batches(X, NB), batches(Z, NB)
        x_full, out_full = batches(x, NB - 1), batches(out, NB - 1)
        x_last = x[(NB - 1) * B:N, :].rearrange("(p g) f -> p (g f)", g=G)
        out_last = out[(NB - 1) * B:N, :].rearrange("(p g) f -> p (g f)", g=G)

        big = sb("big", [P, T * D])
        zin, xin, vv, xo, xT, zo = (big[:, i * U * ED:(i + 1) * U * ED].rearrange("p (s e) -> p s e", s=U)
                                    for i in range(6))
        messages = big[:, :].rearrange("p (g e) -> p g e", e=K * D)
        gat = sb("gathered_rows", [P, U, K * D])
        gatT = sb("gathered_rows_T", [P, 2, K * D])
        relmsg = sb("relation_messages", [P, 2, K * D])
        same = sb("same_target", [P, 2, K, K * P])
        sca = gat
        hl = same[:, :, :, :].rearrange("p a k e -> p (a k e)").rearrange("p (s e) -> p s e", s=U)
        gidx = sb("gather_index_slot", [P, U, K], I32)
        sidx = sb("scatter_index_slot", [P, U, K], I32)
        kslot = sb("key_slot", [P, U, K])

        W0n, Wln = sb("W0_natural", [P, D]), sb("Wl_natural", [P, D])
        W0s, W1s, W2s, W3s, Wls = (sb(f"weight_{n}", [P, D]) for n in ("0", "1", "2", "3", "l"))
        Wrs = sb("weight_relations", [P, R * D])
        b0B, b2B, blB, g4B, e4B = (sb(f"row_{n}", [P, D]) for n in ("b0", "b2", "bl", "gam4", "bet4"))
        b1C, b3C, g3C, e3C = (sb(f"col_{n}", [P, 1]) for n in ("b1", "b3", "gam3", "bet3"))
        bnA, bnB = sb("bn_scale", [P, 1]), sb("bn_shift", [P, 1])
        bna, bnb = sb("bn_scale_leaky", [P, 1]), sb("bn_shift_leaky", [P, 1])
        ident = sb("ident", [P, P])
        eps = sb("eps", [P, 1])
        raw = sb("edges_raw", [P, 3, T], I32)
        key = sb("edges_key", [P, 2, T])
        eidx = sb("edges_index", [P, 2, T], I32)
        row = sb("edges_row", [P, 2, T])
        col = sb("edges_col", [P, 2, T])
        tmpi = sb("tmp_int", [P, 2, 2, T], I32)
        later = sb("later_same_target", [P, 2, T])
        latg = sb("later_slot", [P, U, 2, K])
        sidxt = sb("scatter_index", [P, 2, T], I32)
        trash_i = sb("trash_int", [P, T], I32)
        trash = sb("trash", [P, T])
        tgt = sb("target", [P, T])
        typm = sb("type_mask", [P, R, T])
        after = sb("after_mask", [P, P])
        scr = sb("scratch", [P, K * P])
        ci = sb("column_int", [P, 2 * HC], I32)
        ch = sb("column_half", [P, 2 * HC], F16)
        ohp = sb("onehot_row", [P, U, P], F16)
        ohc = sb("onehot_col", [P, U, 2 * HC], F16)
        cS, cD = sb("rsqrt_deg_src", [P, 2 * HC]), sb("rsqrt_deg_dst", [P, 2 * HC])
        dg3, rd3 = sb("deg_in", [P, 2 * HC]), sb("recip_deg_in", [P, 2 * HC])
        norms = [dict(six=sb(f"bn_six_{i}", [P, U, G, 6]),
                      **{n: sb(f"{n}_{i}", [P, U, G]) for n in ("mean2", "diff", "var", "sd", "rs", "mean", "shift")})
                 for i in range(2)]
        bns = sb("bn_stats_all", [P, 2 * (NB - 1) + G, 6])
        bnm = sb("bn_mean_var", [P, 2])
        bnt = sb("bn_tmp", [P, 4])

        ps = ctx.enter_context(nc.psum_tensor("ps", [P, 8, 512], F32))

        def pair(i):
            return ps[:, 2 * i:2 * i + 2, :].rearrange("p a (h f) -> p (a h) f", f=D)

        def pair_flat(i):
            return ps[:, 2 * i:2 * i + 2, :].rearrange("p a e -> p (a e)")

        def g3(a):
            return a.rearrange("p (g f) -> p g f", g=G)

        def per_node(table, b):
            return table[:, bass.ds(b * G, G)].unsqueeze(2).to_broadcast([P, G, D])

        def per_feature(r):
            return r[:, :].unsqueeze(1).to_broadcast([P, G, D])

        def known(v):
            return isinstance(v, int)

        def wait(eng, s, v):
            if not known(v) or v > 0:
                eng.wait_ge(s, v)

        def steps(eng, n, skew, body):
            head = min(n, U * -(-(skew + U) // U))
            rounds = (n - head) // U
            for t in range(head):
                body(t, t % U, lambda b: 0 <= b < n)
            if rounds:
                with eng.Fori(0, rounds) as i:
                    for u in range(U):
                        body(i * U + (head + u), u, lambda b: True)
            for t in range(head + rounds * U, n + skew):
                body(t, t % U, lambda b: 0 <= b < n)

        def nth(j, b, s, n=NB, unit=16):
            return j * -(-(n - s) // U) * unit + (b - s) * (unit // U) + unit

        def all_through(eng, ring, j, n=NB, unit=16):
            for s in range(U):
                eng.wait_ge(ring[s], (j + 1) * -(-(n - s) // U) * unit)

        def freed(eng, ring, j, b, s, n=NB, unit=16):
            if not known(b) or b >= U:
                eng.wait_ge(ring[s], nth(j, b - U, s, n, unit))

        def group(layer, b, s):
            return nth(layer, b, s, NG, 16 * K)

        def sems(name):
            return [sem(f"{name}_{s}") for s in range(U)]

        zin_in, xin_in, z_stored, x_stored = sems("zin_in"), sems("xin_in"), sems("z_stored"), sems("x_stored")
        raw_zero = sem("raw_zero")
        consts_in = sem("consts_in")
        N_CONST = 16 + 6
        pool_consts = sem("pool_consts")
        pchain = sem("pool_chain")
        keys_raw = sem("keys_raw")
        keys_padded = sem("keys_padded")
        prep = sem("vector_prep_chain")
        onehot = sem("onehot")
        hist_used = sem("hist_used")
        deg1 = sem("deg_plus_one")
        deg_sqrt = sem("deg_sqrt")
        wT_ps, wT_sb = sem("weights_T_psum"), sem("weights_T_sbuf")
        lat_chain, lat_table = sem("later_chain"), sem("later_table")
        prep_done = sem("prep_done")
        zeros_in = sem("trash_zeroed")
        deg_ready = sem("degrees_ready")
        targets = sem("scatter_indices_ready")
        key_slot = sem("key_slot_in")
        begun = sem("indirect_group_begun")

        gidx_in = sem("gather_index_in")
        gathered = sems("gathered")
        keyR = sem("keyR")
        same_in = sem("same_in")
        grouped = sem("grouped")
        msg_in = sem("message_in")
        sca_in = sem("scatter_rows_in")
        scattered = sem("scattered")
        gatT_ps, gatT_sb, rel_ps, rel_in, rel_chain = (sem(n) for n in (
            "gatheredT_psum", "gatheredT_sbuf", "relations_psum", "relation_msg_in", "relation_chain"))

        def node_pass(name, names, zl=0, xl=0, zs=0, xs=0):
            return dict(zl=zl, xl=xl, zs=zs, xs=xs, **{n: sem(f"{name}_{n}") for n in names.split()})

        p0 = node_pass("p0", "x_T xT_in proj biased z_out", xl=0, zs=0)
        p1 = node_pass("p1", "v ua dva var sd dvb x_out x_T xT_in proj z_out", zl=0, xl=1, zs=1, xs=0)
        p2 = node_pass("p2", "v x_T xT_in proj z_out", zl=1, zs=2)
        p3 = node_pass("p3", "v v_chain ua dva var sd dvb x_out x_T xT_in proj z_out", zl=2, xl=2, zs=3, xs=1)
        p4 = node_pass("p4", "v x_T stats", zl=3)
        p5 = node_pass("p5", "v v_T hT leaky h_back ua dva var sd dvb x_out x_T xT_in proj biased z_out",
                       zl=4, xl=3, zs=4, xs=2)
        p6 = node_pass("p6", "v xb dva var sd fin1 y gam ua var2 sd2 fin2 o_out", zl=5, xl=4, xs=3)
        fin_chain = [sem(f"fin_chain_{i}") for i in range(3)]
        bn_chain, bn_sd, bn_ready = sem("bn_chain"), sem("bn_sd"), sem("bn_ready")

        block = ctx.enter_context(nc.Block())

        def after_p0(e):
            all_through(e, z_stored, p0["zs"])

        def after_edges(e, layer):
            e.wait_ge(scattered, 16 * T * (layer + 1))

        def after_p1(e):
            all_through(e, z_stored, p1["zs"])
            all_through(e, x_stored, p1["xs"])

        def after_p2(e):
            all_through(e, z_stored, p2["zs"])

        def after_p3(e):
            all_through(e, z_stored, p3["zs"])
            all_through(e, x_stored, p3["xs"])

        def after_p5(e):
            all_through(e, z_stored, p5["zs"])
            all_through(e, x_stored, p5["xs"])

        @block.sync
        def _(sp):
            for a, s in ((W0n, W0), (Wln, Wl), (W1s, W1), (W2s, W2), (W3s, W3)):
                sp.dma_start(a[:, :], s[:, :]).then_inc(consts_in, 16)
            sp.dma_start(Wrs[:, :].rearrange("i (r o) -> i r o", r=R),
                         Wr.rearrange("r i o -> i r o")).then_inc(consts_in, 16)
            for a, s in ((b0B, b0), (b2B, b2), (blB, bl), (g4B, gam4), (e4B, bet4)):
                sp.dma_start(a[:, :], s.unsqueeze(0).to_broadcast([P, D])).then_inc(consts_in, 16)
            for a, s in ((b1C, b1), (b3C, b3), (g3C, gam3), (e3C, bet3)):
                sp.dma_start(a[:, :], s.rearrange("(p o) -> p o", o=1)).then_inc(consts_in, 16)
            sp.wait_ge(raw_zero, 1)
            for i, s in enumerate((src, dst, edge_type)):
                sp.dma_start(raw[0:EFULL, i, :], s[0:EFULL * T].rearrange("(p t) -> p t", t=T)).then_inc(consts_in, 16)
                sp.dma_start(raw[EFULL:EFULL + 1, i, 0:EREST], s[EFULL * T:E].unsqueeze(0)).then_inc(consts_in, 16)
            sp.dma_start(Z[NP:NP + TRASH, :].rearrange("(p k) f -> p (k f)", k=K), scr[:, :]).then_inc(zeros_in, 16)

            def load_x(b, s, free, from_input):
                wait(sp, free, b - U + 1)
                if from_input and known(b) and b == NB - 1:
                    sp.dma_start(xin[0:LASTP, s, :], x_last).then_inc(xin_in[s], 16)
                else:
                    sp.dma_start(xin[:, s, :], (x_full if from_input else Xb)[b]).then_inc(xin_in[s], 16)

            def load_z(b, s, free):
                wait(sp, free, b - U + 1)
                sp.dma_start(zin[:, s, :], Zb[b]).then_inc(zin_in[s], 16)

            def load_steps(body):
                steps(sp, NB, 1, lambda t, s, live: body(t - 1, (s - 1) % U) if live(t - 1) else None)

            sp.wait_ge(prep_done, 1)
            load_steps(lambda b, s: load_x(b, s, p0["x_T"], True))
            after_edges(sp, 0)

            def p1_loads(b, s):
                load_z(b, s, p1["v"])
                load_x(b, s, p1["var"], True)
            load_steps(p1_loads)
            after_edges(sp, 1)
            load_steps(lambda b, s: load_z(b, s, p2["v"]))
            after_edges(sp, 2)

            def p3_loads(b, s):
                load_z(b, s, p3["v"])
                load_x(b, s, p3["var"], False)
            load_steps(p3_loads)
            after_edges(sp, 3)
            load_steps(lambda b, s: load_z(b, s, p4["v"]))
            sp.wait_ge(bn_ready, 1)

            def p5_loads(t, s, live):
                if live(t):
                    load_z(t, s, p5["v"])
                if live(t - 4):
                    load_x(t - 4, s, p5["x_out"], False)
            steps(sp, NB, 4, p5_loads)
            after_edges(sp, 4)

            def p6_loads(t, s, live):
                if live(t):
                    load_z(t, s, p6["v"])
                if live(t - 3):
                    load_x(t - 3, (s - 3) % U, p6["ua"], False)
            steps(sp, NB, 3, p6_loads)
            sp.wait_ge(zeros_in, 16)
            all_through(sp, x_stored, p6["xs"])

        @block.gpsimd
        def _(pool):
            n = [0]

            def link(ins):
                n[0] += 1
                ins.then_inc(pchain, 1)
                pool.wait_ge(pchain, n[0])

            link(nc.gpsimd.memset(ident[:, :], 0.0))
            link(nc.gpsimd.affine_select(out=ident[:, :], in_=ident[:, :], compare_op=ALU.not_equal, fill=1.0, base=0,
                                         pattern=[[-1, P]], channel_multiplier=1))
            link(nc.gpsimd.memset(after[:, :], 1.0))
            link(nc.gpsimd.affine_select(out=after[:, :], in_=after[:, :], compare_op=ALU.is_gt, fill=0.0,
                                         base=0, pattern=[[1, P]], channel_multiplier=-1))
            nc.gpsimd.iota(trash_i[:, :], pattern=[[0, NG], [P, K]], base=NP, channel_multiplier=1)
            nc.gpsimd.iota(ci[:, :], pattern=[[1, 2 * HC]], base=0, channel_multiplier=0).then_inc(pool_consts, 1)
            pool.wait_ge(keys_raw, 1)
            for i in range(2):
                last = nc.gpsimd.affine_select(out=key[:, i, :], in_=key[:, i, :], compare_op=ALU.is_ge,
                                               fill=float(N), base=E - 1, pattern=[[-1, T]], channel_multiplier=-T)
            last.then_inc(keys_padded, 1)

            def gather(layer, table, rows):
                def body(t, s, live):
                    base = layer * NG
                    wait(pool, gidx_in, base + t + 1)
                    wait(pool, grouped, base + t - U + 1)
                    pool.sem_inc(begun, 1)
                    for k in range(K):
                        nc.gpsimd.indirect_dma_start(
                            out=gat[:, s, k * D:(k + 1) * D], out_offset=None, in_=rows,
                            in_offset=bass.IndirectOffsetOnAxis(ap=gidx[:, s, k:k + 1], axis=0)).then_inc(gathered[s], 16)
                steps(pool, NG, 0, body)

            def scatter(layer):
                all_through(pool, gathered, layer, NG, 16 * K)
                if layer == 0:
                    pool.wait_ge(zeros_in, 16)

                def body(t, s, live):
                    base = layer * NG
                    wait(pool, sca_in, base + t + 1)
                    wait(pool, scattered, (base + t) * 16 * K)
                    pool.sem_inc(begun, 1)
                    for k in range(K):
                        nc.gpsimd.indirect_dma_start(
                            out=Z[:, :], out_offset=bass.IndirectOffsetOnAxis(ap=sidx[:, s, k:k + 1], axis=0),
                            in_=sca[:, s, k * D:(k + 1) * D], in_offset=None,
                            compute_op=ALU.add).then_inc(scattered, 16)
                steps(pool, NG, 0, body)

            def scale(q, b, s, table, free):
                pool.wait_ge(zin_in[s], nth(q["zl"], b, s))
                wait(pool, free, b - U + 1)
                nc.gpsimd.tensor_tensor(g3(vv[:, s, :]), g3(zin[:, s, :]), per_node(table, b),
                                        ALU.mult).then_inc(q["v"], 1)

            def scale_out(q, b, s, table):
                pool.wait_ge(q["biased"], b + 1)
                nc.gpsimd.tensor_tensor(g3(zo[:, s, :]), g3(zo[:, s, :]), per_node(table, b),
                                        ALU.mult).then_inc(q["z_out"], 1)

            after_p0(pool)
            gather(0, 1, Z[:, :])
            scatter(0)
            steps(pool, NB, 0, lambda t, s, live: scale(p1, t, s, cS, p1["x_out"]))
            after_p1(pool)
            gather(1, 0, Z[:, :])
            scatter(1)
            steps(pool, NB, 0, lambda t, s, live: scale(p2, t, s, cD, p2["x_T"]))
            after_p2(pool)
            gather(2, 0, Z[:, :])
            scatter(2)

            def p3_body(t, s, live):
                pool.wait_ge(zin_in[s], nth(p3["zl"], t, s))
                wait(pool, p3["x_out"], t - U + 1)
                nc.gpsimd.tensor_tensor(g3(vv[:, s, :]), g3(zin[:, s, :]), per_node(cD, t),
                                        ALU.mult).then_inc(p3["v_chain"], 1)
                pool.wait_ge(p3["v_chain"], t + 1)
                nc.gpsimd.tensor_tensor(g3(vv[:, s, :]), g3(vv[:, s, :]), per_feature(b2B),
                                        ALU.add).then_inc(p3["v"], 1)
            steps(pool, NB, 0, p3_body)
            after_p3(pool)
            gather(3, 0, Z[:, :])
            scatter(3)
            steps(pool, NB, 0, lambda t, s, live: scale(p4, t, s, cD, p4["x_T"]))

            def p5_body(t, s, live):
                if live(t - 12):
                    scale_out(p5, t - 12, s, dg3)
                if live(t - 3):
                    b, q = t - 3, (s - 3) % U
                    pool.wait_ge(p5["hT"], b + 1)
                    nc.gpsimd.tensor_tensor(hl[:, q, :], hl[:, q, :], vv[:, q, :], ALU.subtract).then_inc(p5["leaky"], 1)
                if live(t):
                    scale(p5, t, s, cD, p5["leaky"])
            steps(pool, NB, 12, p5_body)
            after_p5(pool)
            gather(4, 0, X[:, :])
            scatter(4)

            def p6_body(t, s, live):
                if live(t - 4):
                    b, q = t - 4, (s - 4) % U
                    pool.wait_ge(p6["y"], b + 1)
                    nc.gpsimd.tensor_tensor(g3(zo[:, q, :]), g3(zo[:, q, :]), per_feature(g4B),
                                            ALU.mult).then_inc(p6["gam"], 1)
                if live(t - 4):
                    b, q = t - 4, (s - 4) % U
                    pool.wait_ge(xin_in[q], nth(p6["xl"], b, q))
                    nc.gpsimd.tensor_tensor(g3(xin[:, q, :]), g3(xin[:, q, :]), per_feature(e4B),
                                            ALU.add).then_inc(p6["xb"], 1)
                if live(t):
                    scale(p6, t, s, rd3, p6["y"])
            steps(pool, NB, 4, p6_body)

        @block.scalar
        def _(act):
            act.wait_ge(wT_ps, 1)
            nc.scalar.activation(W0s[:, :], ps[:, 6, 0:D], ACT.Copy)
            nc.scalar.activation(Wls[:, :], ps[:, 6, D:2 * D], ACT.Copy).then_inc(wT_sb, 1)
            act.wait_ge(deg1, 1)
            nc.scalar.activation(cS[:, :], cS[:, :], ACT.Sqrt).then_inc(deg_sqrt, 1)

            def evac(q, b, s, func, bias):
                act.wait_ge(q["x_T"], b + 1)
                wait(act, q["proj"], b - U + 1)
                if bias is None:
                    bank = 2 if q is p5 else s % 2
                    nc.scalar.activation(xT[:, s, :], pair_flat(bank), func).then_inc(q["xT_in"], 1)
                else:
                    nc.scalar.activation(xT[:, s, :], pair_flat(s % 2), func, bias=bias).then_inc(q["xT_in"], 1)

            def root(q, b, s, norm, var_sem, sd_sem, free):
                act.wait_ge(var_sem, b + 1)
                wait(act, free, b - U + 1)
                nc.scalar.activation(norm["sd"][:, s, :], norm["var"][:, s, :], ACT.Sqrt, bias=eps[:, 0:1],
                                     scale=1.0 / D).then_inc(sd_sem, 1)

            def project_out(q, b, s, table):
                act.wait_ge(q["proj"], b + 1)
                freed(act, z_stored, q["zs"], b, s)
                for g in range(G):
                    last = nc.scalar.activation(zo[:, s, g * D:(g + 1) * D], pair(2 + s % 2)[:, g, :], ACT.Copy,
                                                scale=table[:, bass.ds(b * G + g, 1)])
                last.then_inc(q["z_out"], 1)

            def store_z(q, b, s):
                act.wait_ge(q["z_out"], b + 1)
                act.dma_start(Zb[b], zo[:, s, :]).then_inc(z_stored[s], 16)

            def store_x(q, b, s):
                act.wait_ge(q["x_out"], b + 1)
                act.dma_start(Xb[b], xo[:, s, :]).then_inc(x_stored[s], 16)

            def edges(layer):
                base = layer * NG
                lag = 3 if layer == 4 else 2

                def body(t, s, live):
                    if live(t - lag):
                        b, q = t - lag, (s - lag) % U
                        act.wait_ge(grouped, base + b + 1)
                        nc.scalar.activation(messages[:, bass.ds(b, 1), :].rearrange("p a e -> p (a e)"),
                                             ps[:, 2 + q % 2 if layer < 4 else 2, :], ACT.Copy).then_inc(msg_in, 1)
                    if layer == 4 and live(t - 2):
                        b, q = t - 2, (s - 2) % U
                        act.wait_ge(rel_ps, b + 1)
                        wait(act, grouped, base + b - 2 + 1)
                        for k in range(K):
                            last = nc.scalar.activation(relmsg[:, q % 2, k * D:(k + 1) * D], ps[:, 4 + k, 0:D],
                                                        ACT.Copy, scale=typm[:, 0, bass.ds(b * K + k, 1)])
                        last.then_inc(rel_in, 1)
                    if layer == 4 and live(t - 1):
                        b, q = t - 1, (s - 1) % U
                        act.wait_ge(gatT_ps, b + 1)
                        wait(act, rel_ps, b - 2 + 1)
                        nc.scalar.activation(gatT[:, q % 2, :], ps[:, 3, :], ACT.Copy).then_inc(gatT_sb, 1)
                steps(act, NG, lag, body)
                all_through(act, gathered, layer, NG, 16 * K)
                act.wait_ge(msg_in, base + NG)
                act.wait_ge(targets, min(layer, 1) + 1)

                def copies(t, s, live):
                    wait(act, scattered, (base + t - U + 1) * 16 * K)
                    nc.scalar.activation(sidx[:, s, :], sidxt[:, min(layer, 1), bass.ds(t * K, K)], ACT.Copy)
                    nc.scalar.activation(sca[:, s, :], messages[:, bass.ds(t, 1), :].rearrange("p a e -> p (a e)"),
                                         ACT.Copy).then_inc(sca_in, 1)
                steps(act, NG, 0, copies)

            def p0_body(t, s, live):
                if live(t - 3):
                    store_z(p0, t - 3, (s - 3) % U)
                if live(t):
                    evac(p0, t, s, ACT.Copy, None)
            act.wait_ge(prep_done, 1)
            steps(act, NB, 3, p0_body)
            after_p0(act)
            edges(0)
            act.wait_ge(deg1, 2)
            nc.scalar.activation(cD[:, :], cD[:, :], ACT.Sqrt).then_inc(deg_sqrt, 1)

            def mid(q, table):
                def body(t, s, live):
                    if live(t):
                        root(q, t, s, norms[0], q["var"], q["sd"], q["x_out"])
                    if live(t - 2):
                        evac(q, t - 2, (s - 2) % U, ACT.Copy, None)
                        store_x(q, t - 2, (s - 2) % U)
                    if live(t - 4):
                        project_out(q, t - 4, (s - 4) % U, table)
                        store_z(q, t - 4, (s - 4) % U)
                steps(act, NB, 4, body)
            after_edges(act, 0)
            act.wait_ge(deg_ready, 1)
            mid(p1, cD)
            after_p1(act)
            edges(1)
            after_edges(act, 1)

            def p2_body(t, s, live):
                if live(t):
                    evac(p2, t, s, ACT.Relu, b1C[:, 0:1])
                if live(t - 3):
                    store_z(p2, t - 3, (s - 3) % U)
            steps(act, NB, 3, p2_body)
            after_p2(act)
            edges(2)
            after_edges(act, 2)
            mid(p3, cS)
            after_p3(act)
            edges(3)
            act.wait_ge(bn_chain, 1)
            nc.scalar.activation(bnt[:, 0:1], bnm[:, 1:2], ACT.Sqrt, bias=eps[:, 0:1]).then_inc(bn_sd, 1)
            act.wait_ge(bn_ready, 1)

            def p5_body(t, s, live):
                if live(t - 9):
                    evac(p5, t - 9, (s - 9) % U, ACT.Copy, None)
                if live(t - 2):
                    b, q = t - 2, (s - 2) % U
                    act.wait_ge(p5["v_T"], b + 1)
                    wait(act, p5["h_back"], b - U + 1)
                    nc.scalar.activation(hl[:, q, :], pair_flat(0), ACT.Relu, bias=bnB[:, 0:1], scale=bnA[:, 0:1])
                    nc.scalar.activation(vv[:, q, :], pair_flat(0), ACT.Relu, bias=bnb[:, 0:1],
                                         scale=bna[:, 0:1]).then_inc(p5["hT"], 1)
                if live(t - 6):
                    root(p5, t - 6, (s - 6) % U, norms[0], p5["var"], p5["sd"], p5["x_out"])
                if live(t - 8):
                    store_x(p5, t - 8, s)
                if live(t - 13):
                    store_z(p5, t - 13, (s - 13) % U)
            steps(act, NB, 13, p5_body)
            after_p5(act)
            edges(4)
            after_edges(act, 4)

            def normalise(dst_, src_, norm, s):
                for g in range(G):
                    last = nc.scalar.activation(dst_[:, s, g * D:(g + 1) * D], src_[:, s, g * D:(g + 1) * D],
                                                ACT.Identity, bias=norm["shift"][:, s, g:g + 1],
                                                scale=norm["rs"][:, s, g:g + 1])
                return last

            def p6_body(t, s, live):
                if live(t - 3):
                    b, q = t - 3, (s - 3) % U
                    act.wait_ge(p6["fin1"], b + 1)
                    wait(act, p6["ua"], b - U + 1)
                    normalise(zo, vv, norms[0], q).then_inc(p6["y"], 1)
                if live(t - 8):
                    b, q = t - 8, (s - 8) % U
                    act.wait_ge(p6["fin2"], b + 1)
                    freed(act, x_stored, p6["xs"], b, q)
                    normalise(xo, xT, norms[1], q).then_inc(p6["o_out"], 1)
                    act.wait_ge(p6["o_out"], b + 1)
                    if known(b) and b == NB - 1:
                        act.dma_start(out_last, xo[0:LASTP, q, :]).then_inc(x_stored[q], 16)
                    else:
                        act.dma_start(out_full[b], xo[:, q, :]).then_inc(x_stored[q], 16)
                if live(t - 6):
                    root(p6, t - 6, (s - 6) % U, norms[1], p6["var2"], p6["sd2"], p6["fin2"])
                if live(t - 1):
                    root(p6, t - 1, (s - 1) % U, norms[0], p6["var"], p6["sd"], p6["fin1"])
            steps(act, NB, 8, p6_body)

        @block.vector
        def _(dve):
            n = [0]

            def link(ins):
                n[0] += 1
                ins.then_inc(prep, 1)
                dve.wait_ge(prep, n[0])

            nc.vector.memset(raw[:, :, :], 0)
            nc.vector.memset(eps[:, :], EPS)
            nc.vector.memset(latg[:, :, :, :], 0.0)
            nc.vector.memset(scr[:, :], 0.0).then_inc(raw_zero, 1)
            dve.wait_ge(consts_in, 16 * (15 + 6))
            nc.vector.tensor_copy(key[:, :, :], raw[:, 0:2, :]).then_inc(keys_raw, 1)
            for r in range(R):
                nc.vector.tensor_scalar(typm[:, r, :], raw[:, 2, :], float(r), None, ALU.is_equal)
            dve.wait_ge(pool_consts, 1)
            nc.vector.tensor_copy(trash[:, :], trash_i[:, :])
            nc.vector.tensor_copy(ch[:, :], ci[:, :])
            dve.wait_ge(keys_padded, 1)
            link(nc.vector.tensor_copy(eidx[:, :, :], key[:, :, :]))
            nc.vector.tensor_scalar(tmpi[:, 0, :, :], eidx[:, :, :], 3, P - 1, ALU.logical_shift_right,
                                    ALU.bitwise_and)
            nc.vector.tensor_scalar(tmpi[:, 1, :, :], eidx[:, :, :], 10, 3, ALU.logical_shift_right,
                                    ALU.logical_shift_left)
            link(nc.vector.tensor_copy(later[:, :, :], key[:, :, :]))
            link(nc.vector.tensor_copy(row[:, :, :], tmpi[:, 0, :, :]))
            link(nc.vector.tensor_copy(col[:, :, :], tmpi[:, 1, :, :]))
            link(nc.vector.tensor_scalar(tmpi[:, 0, :, :], eidx[:, :, :], G - 1, None, ALU.bitwise_and))
            link(nc.vector.tensor_copy(later[:, :, :], tmpi[:, 0, :, :]))
            link(nc.vector.tensor_tensor(col[:, :, :], col[:, :, :], later[:, :, :], ALU.add))

            def one_hots(i):
                def body(t, s, live):
                    wait(dve, hist_used, i * T + t - U + 1)
                    nc.vector.tensor_scalar(ohp[:, s, :], ch[:, 0:P], row[:, i, bass.ds(t, 1)], None, ALU.is_equal)
                    nc.vector.tensor_scalar(ohc[:, s, :], ch[:, :], col[:, i, bass.ds(t, 1)], None,
                                            ALU.is_equal).then_inc(onehot, 1)
                steps(dve, T, 0, body)
                dve.wait_ge(hist_used, (i + 1) * T)

            def hist(i):
                return ps[:, 4 + 2 * i:6 + 2 * i, 0:HC]

            def halves(a):
                return a[:, :].rearrange("p (a c) -> p a c", a=2)

            one_hots(0)
            nc.vector.tensor_scalar(halves(cS), hist(0), 1.0, None, ALU.add).then_inc(deg1, 1)
            dve.wait_ge(deg_sqrt, 1)
            nc.vector.reciprocal(cS[:, :], cS[:, :]).then_inc(prep_done, 1)

            def dst_degrees():
                one_hots(1)
                nc.vector.tensor_scalar(halves(cD), hist(1), 1.0, None, ALU.add).then_inc(deg1, 1)
                link(nc.vector.tensor_scalar(halves(dg3), hist(1), 1.0, None, ALU.max))
                nc.vector.reciprocal(rd3[:, :], dg3[:, :])
                dve.wait_ge(deg_sqrt, 2)
                nc.vector.reciprocal(cD[:, :], cD[:, :]).then_inc(deg_ready, 1)

            def scatter_indices(i):
                dve.wait_ge(lat_table, (i + 1) * NG)
                link(nc.vector.tensor_scalar(later[:, i, :], later[:, i, :], 1.0, None, ALU.min))
                link(nc.vector.tensor_tensor(tgt[:, :], trash[:, :], key[:, i, :], ALU.subtract))
                link(nc.vector.tensor_tensor(tgt[:, :], tgt[:, :], later[:, i, :], ALU.mult))
                link(nc.vector.tensor_tensor(tgt[:, :], tgt[:, :], key[:, i, :], ALU.add))
                nc.vector.tensor_copy(sidxt[:, i, :], tgt[:, :]).then_inc(targets, 1)

            def edges(layer, gi, ki):
                base = layer * NG

                def body(t, s, live):
                    if live(t):
                        freed(dve, gathered, layer, t, s, NG, 16 * K)
                        nc.vector.tensor_copy(gidx[:, s, :], eidx[:, gi, bass.ds(t * K, K)]).then_inc(gidx_in, 1)
                        wait(dve, keyR, base + t - U + 1)
                        nc.vector.tensor_copy(kslot[:, s, :], key[:, ki, bass.ds(t * K, K)]).then_inc(key_slot, 1)
                    if live(t - 1):
                        b, q = t - 1, (s - 1) % U
                        dve.wait_ge(keyR, base + b + 1)
                        wait(dve, grouped, base + b - 2 + 1)
                        for k in range(K):
                            mine = key[:, ki, bass.ds(b * K + k, 1)]
                            if layer > 1:
                                last = nc.vector.tensor_scalar(same[:, q % 2, k, k * P:], ps[:, q % 2, k * P:],
                                                               mine, None, ALU.is_equal)
                                continue
                            nc.vector.scalar_tensor_tensor(
                                out=scr[:, k * P:(k + 1) * P], in0=ps[:, q % 2, k * P:(k + 1) * P], scalar=mine, in1=after[:, :],
                                op0=ALU.is_equal, op1=ALU.mult, accum_out=latg[:, q, 0, k:k + 1])
                            last = nc.vector.tensor_scalar(same[:, q % 2, k, k * P:(k + 1) * P],
                                                           ps[:, q % 2, k * P:(k + 1) * P], mine, None, ALU.is_equal)
                            if k < K - 1:
                                last = nc.vector.tensor_scalar(
                                    same[:, q % 2, k, (k + 1) * P:], ps[:, q % 2, (k + 1) * P:], mine, 0.0,
                                    ALU.is_equal, ALU.add, accum_out=latg[:, q, 1, k:k + 1])
                        last.then_inc(same_in, 1)
                        if layer <= 1:
                            dve.wait_ge(same_in, base + b + 1)
                            nc.vector.tensor_tensor(later[:, ki, bass.ds(b * K, K)], latg[:, q, 0, :],
                                                    latg[:, q, 1, :], ALU.add).then_inc(lat_table, 1)
                    if layer == 4 and live(t - 2):
                        b, q = t - 2, (s - 2) % U
                        dve.wait_ge(rel_in, b + 1)
                        for r in range(1, R):
                            if r > 1:
                                dve.wait_ge(rel_chain, b * (R - 1) + (r - 1))
                            for k in range(K):
                                m = relmsg[:, q % 2, k * D:(k + 1) * D]
                                last = nc.vector.scalar_tensor_tensor(
                                    out=m, in0=ps[:, 4 + k, r * D:(r + 1) * D],
                                    scalar=typm[:, r, bass.ds(b * K + k, 1)], in1=m, op0=ALU.mult, op1=ALU.add)
                            last.then_inc(rel_chain, 1)
                steps(dve, NG, 2 if layer == 4 else 1, body)

            def ln_stats(a, b, s, norm, chain, done):
                six, mean2, diff, var = norm["six"], norm["mean2"], norm["diff"], norm["var"]
                for g in range(G):
                    last = nc.vector.bn_stats(six[:, s, g, :], a[:, g, :])
                last.then_inc(chain, 1)
                dve.wait_ge(chain, b * 3 + 1)
                nc.vector.tensor_tensor(diff[:, s, :], six[:, s, :, 1], six[:, s, :, 4], ALU.subtract)
                nc.vector.tensor_tensor(mean2[:, s, :], six[:, s, :, 1], six[:, s, :, 4], ALU.add)
                nc.vector.tensor_tensor(var[:, s, :], six[:, s, :, 2], six[:, s, :, 5], ALU.add).then_inc(chain, 1)
                dve.wait_ge(chain, b * 3 + 2)
                nc.vector.tensor_tensor(diff[:, s, :], diff[:, s, :], diff[:, s, :], ALU.mult)
                nc.vector.tensor_scalar(norm["mean"][:, s, :], mean2[:, s, :], 0.5, None, ALU.mult).then_inc(chain, 1)
                dve.wait_ge(chain, b * 3 + 3)
                nc.vector.scalar_tensor_tensor(out=var[:, s, :], in0=diff[:, s, :], scalar=D / 4.0, in1=var[:, s, :],
                                               op0=ALU.mult, op1=ALU.add).then_inc(done, 1)

            def norm_out(q, b, s, a=vv):
                norm = norms[0]
                dve.wait_ge(q["sd"], b + 1)
                nc.vector.reciprocal(norm["rs"][:, s, :], norm["sd"][:, s, :]).then_inc(q["dvb"], 1)
                wait(dve, q["x_T"], b - U + 1)
                freed(dve, x_stored, q["xs"], b, s)
                dve.wait_ge(q["dvb"], b + 1)
                for g in range(G):
                    last = nc.vector.tensor_scalar(xo[:, s, g * D:(g + 1) * D], a[:, s, g * D:(g + 1) * D],
                                                   norm["mean"][:, s, g:g + 1], norm["rs"][:, s, g:g + 1],
                                                   ALU.subtract, ALU.mult)
                last.then_inc(q["x_out"], 1)

            def biased(q, b, s, bias, bank):
                dve.wait_ge(q["proj"], b + 1)
                freed(dve, z_stored, q["zs"], b, s)
                nc.vector.tensor_tensor(g3(zo[:, s, :]), pair(bank), per_feature(bias), ALU.add).then_inc(q["biased"], 1)

            def p0_body(t, s, live):
                biased(p0, t, s, b0B, 2 + s % 2)
                dve.wait_ge(p0["biased"], t + 1)
                nc.vector.tensor_tensor(g3(zo[:, s, :]), g3(zo[:, s, :]), per_node(cS, t), ALU.mult).then_inc(p0["z_out"], 1)
            steps(dve, NB, 0, p0_body)
            after_p0(dve)
            edges(0, 1, 0)
            scatter_indices(0)
            dst_degrees()
            after_edges(dve, 0)

            def p1_body(t, s, live):
                if live(t):
                    dve.wait_ge(p1["v"], t + 1)
                    dve.wait_ge(xin_in[s], nth(p1["xl"], t, s))
                    nc.vector.scalar_tensor_tensor(out=vv[:, s, :], in0=vv[:, s, :], scalar=0.0, in1=xin[:, s, :],
                                                   op0=ALU.max, op1=ALU.add).then_inc(p1["ua"], 1)
                    dve.wait_ge(p1["ua"], t + 1)
                    ln_stats(g3(vv[:, s, :]), t, s, norms[0], p1["dva"], p1["var"])
                if live(t - 1):
                    norm_out(p1, t - 1, (s - 1) % U)
            steps(dve, NB, 1, p1_body)
            after_p1(dve)
            edges(1, 0, 1)
            scatter_indices(1)
            after_edges(dve, 1)

            def p2_body(t, s, live):
                dve.wait_ge(p2["proj"], t + 1)
                freed(dve, z_stored, p2["zs"], t, s)
                nc.vector.tensor_tensor(g3(zo[:, s, :]), pair(2 + s % 2), per_node(cD, t),
                                        ALU.mult).then_inc(p2["z_out"], 1)
            steps(dve, NB, 0, p2_body)
            after_p2(dve)
            edges(2, 0, 1)
            after_edges(dve, 2)

            def p3_body(t, s, live):
                if live(t):
                    dve.wait_ge(p3["v"], t + 1)
                    dve.wait_ge(xin_in[s], nth(p3["xl"], t, s))
                    nc.vector.tensor_tensor(vv[:, s, :], vv[:, s, :], xin[:, s, :], ALU.add).then_inc(p3["ua"], 1)
                    dve.wait_ge(p3["ua"], t + 1)
                    ln_stats(g3(vv[:, s, :]), t, s, norms[0], p3["dva"], p3["var"])
                if live(t - 1):
                    norm_out(p3, t - 1, (s - 1) % U)
            steps(dve, NB, 1, p3_body)
            after_p3(dve)
            edges(3, 0, 1)
            after_edges(dve, 3)

            def p4_body(t, s, live):
                dve.wait_ge(p4["x_T"], t + 1)
                if known(t) and t == NB - 1:
                    for g in range(G):
                        last = nc.vector.bn_stats(bns[:, 2 * (NB - 1) + g, :], pair(s)[:, g, 0:LASTP])
                else:
                    for h in range(2):
                        last = nc.vector.bn_stats(bns[:, bass.ds(t * 2 + h, 1), :].rearrange("p a e -> p (a e)"),
                                                  ps[:, 2 * s + h, :])
                last.then_inc(p4["stats"], 1)
            steps(dve, NB - 1, 0, p4_body)
            p4_body(NB - 1, (NB - 1) % U, None)
            dve.wait_ge(p4["stats"], NB)
            nc.vector.bn_aggr(bnm[:, :], bns[:, :, :].rearrange("p a e -> p (a e)")).then_inc(bn_chain, 1)
            dve.wait_ge(bn_chain, 1)
            nc.vector.tensor_tensor(bnt[:, 1:2], bnm[:, 0:1], b3C[:, :], ALU.add).then_inc(bn_chain, 1)
            dve.wait_ge(bn_sd, 1)
            nc.vector.reciprocal(bnt[:, 2:3], bnt[:, 0:1]).then_inc(bn_chain, 1)
            dve.wait_ge(bn_chain, 3)
            nc.vector.tensor_tensor(bnA[:, :], bnt[:, 2:3], g3C[:, :], ALU.mult).then_inc(bn_chain, 1)
            nc.vector.tensor_tensor(bnt[:, 3:4], b3C[:, :], bnt[:, 1:2], ALU.subtract).then_inc(bn_chain, 1)
            dve.wait_ge(bn_chain, 5)
            nc.vector.tensor_tensor(bnB[:, :], bnt[:, 3:4], bnA[:, :], ALU.mult).then_inc(bn_chain, 1)
            dve.wait_ge(bn_chain, 6)
            nc.vector.tensor_tensor(bnB[:, :], bnB[:, :], e3C[:, :], ALU.add).then_inc(bn_chain, 1)
            dve.wait_ge(bn_chain, 7)
            nc.vector.tensor_scalar(bna[:, :], bnA[:, :], -0.01, None, ALU.mult)
            nc.vector.tensor_scalar(bnb[:, :], bnB[:, :], -0.01, None, ALU.mult).then_inc(bn_ready, 1)

            def p5_body(t, s, live):
                if live(t - 11):
                    biased(p5, t - 11, (s - 11) % U, blB, 3)
                if live(t - 5):
                    b, q = t - 5, (s - 5) % U
                    dve.wait_ge(p5["h_back"], b + 1)
                    dve.wait_ge(xin_in[q], nth(p5["xl"], b, q))
                    nc.vector.tensor_tensor(g3(xin[:, q, :]), pair(1), g3(xin[:, q, :]), ALU.add).then_inc(p5["ua"], 1)
                if live(t - 7):
                    norm_out(p5, t - 7, (s - 7) % U, xin)
                if live(t - 5):
                    b, q = t - 5, (s - 5) % U
                    dve.wait_ge(p5["ua"], b + 1)
                    ln_stats(g3(xin[:, q, :]), b, q, norms[0], p5["dva"], p5["var"])
            steps(dve, NB, 11, p5_body)
            after_p5(dve)
            edges(4, 0, 1)
            after_edges(dve, 4)

            def scale_shift(norm, s, sd_sem, chain, b, done):
                dve.wait_ge(sd_sem, b + 1)
                nc.vector.reciprocal(norm["rs"][:, s, :], norm["sd"][:, s, :]).then_inc(chain, 1)
                dve.wait_ge(chain, b + 1)
                nc.vector.scalar_tensor_tensor(out=norm["shift"][:, s, :], in0=norm["mean"][:, s, :], scalar=-1.0,
                                               in1=norm["rs"][:, s, :], op0=ALU.mult, op1=ALU.mult).then_inc(done, 1)

            def p6_body(t, s, live):
                if live(t - 2):
                    b, q = t - 2, (s - 2) % U
                    wait(dve, p6["y"], b - U + 1)
                    scale_shift(norms[0], q, p6["sd"], fin_chain[0], b, p6["fin1"])
                if live(t - 7):
                    b, q = t - 7, (s - 7) % U
                    wait(dve, p6["o_out"], b - U + 1)
                    scale_shift(norms[1], q, p6["sd2"], fin_chain[1], b, p6["fin2"])
                if live(t - 1):
                    b, q = t - 1, (s - 1) % U
                    dve.wait_ge(p6["v"], b + 1)
                    wait(dve, p6["fin1"], b - U + 1)
                    ln_stats(g3(vv[:, q, :]), b, q, norms[0], p6["dva"], p6["var"])
                if live(t - 5):
                    b, q = t - 5, (s - 5) % U
                    dve.wait_ge(p6["gam"], b + 1)
                    dve.wait_ge(p6["xb"], b + 1)
                    wait(dve, p6["o_out"], b - U + 1)
                    nc.vector.tensor_tensor(xT[:, q, :], zo[:, q, :], xin[:, q, :], ALU.add).then_inc(p6["ua"], 1)
                    dve.wait_ge(p6["ua"], b + 1)
                    ln_stats(g3(xT[:, q, :]), b, q, norms[1], fin_chain[2], p6["var2"])
            steps(dve, NB, 7, p6_body)

        @block.tensor
        def _(pe):
            pe.wait_ge(consts_in, 16 * (15 + 6))
            pe.wait_ge(pool_consts, 1)
            nc.tensor.transpose(ps[:, 6, 0:D], W0n[:, :], ident[:, :])
            nc.tensor.transpose(ps[:, 6, D:2 * D], Wln[:, :], ident[:, :]).then_inc(wT_ps, 1)

            def histogram(i):
                def count(t, s, first, final):
                    pe.wait_ge(onehot, i * T + t + 1)
                    for h in range(2):
                        last = nc.tensor.matmul(ps[:, 4 + 2 * i + h, 0:HC], ohp[:, s, :],
                                                ohc[:, s, h * HC:(h + 1) * HC], start=first, stop=final)
                    last.then_inc(hist_used, 1)
                for t in range(U):
                    count(t, t, t == 0, False)
                with pe.Fori(0, T // U - 2) as j:
                    for u in range(U):
                        count(j * U + (U + u), u, False, False)
                for t in range(T - U, T):
                    count(t, t % U, False, t == T - 1)
            histogram(0)

            def key_rows(s, bank, done):
                for k in range(K):
                    last = nc.tensor.transpose(ps[:, bank, k * P:(k + 1) * P],
                                               kslot[:, s, k:k + 1].to_broadcast([P, P]), ident[:, :])
                last.then_inc(done, 1)

            pe.wait_ge(prep_done, 1)

            def transpose_batch(a, bank, done):
                for g in range(G):
                    last = nc.tensor.transpose(pair(bank)[:, g, :], a[:, g * D:(g + 1) * D], ident[:, :])
                last.then_inc(done, 1)

            def project(q, b, s, weight, bank, free, lag):
                pe.wait_ge(q["xT_in"], b + 1)
                wait(pe, free, b - lag + 1)
                for g in range(G):
                    last = nc.tensor.matmul(pair(bank)[:, g, :], xT[:, s, g * D:(g + 1) * D], weight[:, :],
                                            start=True, stop=True)
                last.then_inc(q["proj"], 1)

            def edges(layer, ki):
                base = layer * NG
                lag = 3 if layer == 4 else 2

                def body(t, s, live):
                    if live(t - lag):
                        b, q = t - lag, (s - lag) % U
                        if layer == 4:
                            pe.wait_ge(rel_chain, (b + 1) * (R - 1))
                            rows, bank = relmsg[:, q % 2, :], 2
                            wait(pe, msg_in, base + b)
                        else:
                            pe.wait_ge(gathered[q], group(layer, b, q))
                            rows, bank = gat[:, q, :], 2 + q % 2
                            wait(pe, msg_in, base + b - 2 + 1)
                        pe.wait_ge(same_in, base + b + 1)
                        for j in range(K):
                            for k in range(j + 1):
                                last = nc.tensor.matmul(ps[:, bank, j * D:(j + 1) * D],
                                                        same[:, q % 2, k, j * P:(j + 1) * P],
                                                        rows[:, k * D:(k + 1) * D], start=k == 0, stop=k == j)
                        last.then_inc(grouped, 1)
                    if layer == 4 and live(t - 2):
                        b, q = t - 2, (s - 2) % U
                        pe.wait_ge(gatT_sb, b + 1)
                        wait(pe, rel_chain, b * (R - 1))
                        for k in range(K):
                            last = nc.tensor.matmul(ps[:, 4 + k, 0:R * D], gatT[:, q % 2, k * P:(k + 1) * P],
                                                    Wrs[:, :], start=True, stop=True)
                        last.then_inc(rel_ps, 1)
                    if layer == 4 and live(t - 1):
                        b, q = t - 1, (s - 1) % U
                        pe.wait_ge(gathered[q], group(layer, b, q))
                        wait(pe, gatT_sb, b)
                        for k in range(K):
                            last = nc.tensor.transpose(ps[:, 3, k * P:(k + 1) * P], gat[:, q, k * D:(k + 1) * D],
                                                       ident[:, :])
                        last.then_inc(gatT_ps, 1)
                    if live(t):
                        wait(pe, same_in, base + t - 2 + 1)
                        if layer <= 1:
                            wait(pe, lat_table, base + t - 2 + 1)
                        pe.wait_ge(key_slot, base + t + 1)
                        key_rows(s, s % 2, keyR)
                steps(pe, NG, lag, body)

            def plain(q, a, weight, free):
                def body(t, s, live):
                    if live(t):
                        a(t, s)
                        wait(pe, q["xT_in"], t - 2 + 1)
                        transpose_batch(ring(q)[:, s, :], s % 2, q["x_T"])
                    if live(t - 2):
                        project(q, t - 2, (s - 2) % U, weight, 2 + s % 2, free, 2)
                steps(pe, NB, 2, body)

            def ring(q):
                return xin if q is p0 else vv if q is p2 else xo

            plain(p0, lambda t, s: pe.wait_ge(xin_in[s], nth(p0["xl"], t, s)), W0s, p0["biased"])
            after_p0(pe)
            edges(0, 0)
            histogram(1)
            after_edges(pe, 0)
            plain(p1, lambda t, s: pe.wait_ge(p1["x_out"], t + 1), W1s, p1["z_out"])
            after_p1(pe)
            edges(1, 1)
            after_edges(pe, 1)
            plain(p2, lambda t, s: pe.wait_ge(p2["v"], t + 1), W2s, p2["z_out"])
            after_p2(pe)
            edges(2, 1)
            after_edges(pe, 2)
            plain(p3, lambda t, s: pe.wait_ge(p3["x_out"], t + 1), W3s, p3["z_out"])
            after_p3(pe)
            edges(3, 1)
            after_edges(pe, 3)

            def p4_body(t, s, live):
                pe.wait_ge(p4["v"], t + 1)
                wait(pe, p4["stats"], t - U + 1)
                transpose_batch(vv[:, s, :], s, p4["x_T"])
            steps(pe, NB, 0, p4_body)
            pe.wait_ge(bn_ready, 1)

            def p5_body(t, s, live):
                if live(t - 8):
                    pe.wait_ge(p5["x_out"], t - 8 + 1)
                    wait(pe, p5["xT_in"], t - 8)
                    transpose_batch(xo[:, s, :], 2, p5["x_T"])
                if live(t - 10):
                    project(p5, t - 10, (s - 10) % U, Wls, 3, p5["biased"], 1)
                if live(t - 4):
                    pe.wait_ge(p5["leaky"], t - 4 + 1)
                    wait(pe, p5["ua"], t - 4)
                    transpose_batch(hl[:, s, :], 1, p5["h_back"])
                if live(t - 1):
                    b, q = t - 1, (s - 1) % U
                    pe.wait_ge(p5["v"], b + 1)
                    wait(pe, p5["hT"], b)
                    transpose_batch(vv[:, q, :], 0, p5["v_T"])
            steps(pe, NB, 10, p5_body)
            after_p5(pe)
            edges(4, 1)


_INS = ['x', 'src', 'dst', 'edge_type_3', 'L0_gnn_W', 'L0_gnn_b', 'L1_gnn_W1', 'L1_gnn_b1', 'L1_gnn_W2', 'L1_gnn_b2',
        'L2_gnn_W', 'L2_gnn_b', 'L2_gnn_gamma', 'L2_gnn_beta', 'L3_gnn_relation_weights', 'L3_gnn_lin_w',
        'L3_gnn_lin_b', 'L3_gnn_ln_gamma', 'L3_gnn_ln_beta']


def kernel(**inputs):
    import numpy as _np
    import concourse.bacc as _bacc
    from concourse import mybir as _mybir
    from concourse.bass_utils import run_bass_kernel_spmd as _run

    nc = _bacc.Bacc("TRN2", target_bir_lowering=False, num_devices=1)
    arrays, args = {}, []
    for name in _INS:
        a = _np.ascontiguousarray(inputs[name])
        arrays[f"in_{name}_dram"] = a
        args.append(nc.dram_tensor(f"in_{name}_dram", a.shape, _mybir.dt.from_np(a.dtype), kind="ExternalInput").ap())
    args.append(nc.dram_tensor("out_dram", (N, D), F32, kind="ExternalOutput").ap())
    build(nc, *args)
    r = _run(nc, [arrays], core_ids=[0])
    return r.results[0]["out_dram"]
```

```python
import numpy as np
import concourse.bass as bass
from concourse import mybir
from concourse.alu_op_type import AluOpType as ALU
from contextlib import ExitStack

F32 = mybir.dt.float32
F16 = mybir.dt.float16
BF16 = mybir.dt.bfloat16
I32 = mybir.dt.int32
ACT = mybir.ActivationFunctionType

P = 128
N = 100000
D = 128
E = 25000
R = 3
G = 8
B = P * G
NB = -(-N // B)
NP = NB * B
LASTP = (N - (NB - 1) * B) // G
ED = G * D
T = -(-E // P)
EFULL = E // T
EREST = E - EFULL * T
K = 2
NG = T // K
TT = 2 * K
TRASH = TT * P
HC = NB * G // 2
U = 4
UE = 8
M = 4
EPS = 1e-5
assert T % TT == 0 and LASTP * G + (NB - 1) * B == N and (T - EREST) > 0


def build(nc, x, src, dst, edge_type, W0, b0, W1, b1, W2, b2, W3, b3, gam3, bet3, Wr, Wl, bl, gam4, bet4, out):
    ctx = ExitStack()
    with ctx:
        def sb(name, shape, dt=F32):
            return ctx.enter_context(nc.sbuf_tensor(name, shape, dt))

        def sem(name):
            return ctx.enter_context(nc.semaphore(name))

        X = nc.dram_tensor("node_state", (NP, D), F32, kind="Internal").ap()
        Z = nc.dram_tensor("edge_sums", (NP + TRASH, D), F32, kind="Internal").ap()

        def batches(a, n):
            return a[0:n * B, :].rearrange("(b p g) f -> b p (g f)", p=P, g=G)

        Xb, Zb = batches(X, NB), batches(Z, NB)
        x_full, out_full = batches(x, NB - 1), batches(out, NB - 1)
        x_last = x[(NB - 1) * B:N, :].rearrange("(p g) f -> p (g f)", g=G)
        out_last = out[(NB - 1) * B:N, :].rearrange("(p g) f -> p (g f)", g=G)

        big = sb("big", [P, T * D])
        zin, xin, vv, xo, xT, zo = (big[:, i * U * ED:(i + 1) * U * ED].rearrange("p (s e) -> p s e", s=U)
                                    for i in range(6))
        UL = 2 * U
        zin6, xin6 = (big[:, i * UL * ED:(i + 1) * UL * ED].rearrange("p (s e) -> p s e", s=UL) for i in range(2))
        zo6, xo6 = (big[:, (4 + i) * U * ED:(5 + i) * U * ED].rearrange("p (s e) -> p s e", s=U) for i in range(2))
        messages = big[:, :].rearrange("p (g e) -> p g e", e=K * D)
        gat = sb("gathered_rows", [P, UE, K * D])
        gatT = sb("gathered_rows_T", [P, M, K * D])
        relmsg = sb("relation_messages", [P, M, K * D])
        matrices = sb("same_target", [P, 2 * M * K * K * P])
        same, carry = (matrices[:, i * M * K * K * P:(i + 1) * M * K * K * P].rearrange(
            "p (a k e) -> p a k e", a=M, k=K) for i in range(2))
        sca = gat
        hl = matrices[:, :].rearrange("p (s e) -> p s e", s=U)
        gidx = sb("gather_index_slot", [P, UE, K], I32)
        sidx = sb("scatter_index_slot", [P, UE, K], I32)
        kslot = sb("key_slot", [P, UE, K])

        W0n, Wln = sb("W0_natural", [P, D]), sb("Wl_natural", [P, D])
        W0s, W1s, W2s, W3s, Wls = (sb(f"weight_{n}", [P, D]) for n in ("0", "1", "2", "3", "l"))
        Wrs = sb("weight_relations", [P, R * D])
        b0B, b2B, blB, g4B, e4B = (sb(f"row_{n}", [P, D]) for n in ("b0", "b2", "bl", "gam4", "bet4"))
        b1C, b3C, g3C, e3C = (sb(f"col_{n}", [P, 1]) for n in ("b1", "b3", "gam3", "bet3"))
        bl_parts, bl_rows, ones = sb("bl_parts", [P, 3, D], BF16), sb("bl_rows", [P, D], BF16), sb("ones", [P, P], BF16)
        bl_rest = sb("bl_rest", [P, 2, D])
        bnA, bnB = sb("bn_scale", [P, 1]), sb("bn_shift", [P, 1])
        bna, bnb = sb("bn_scale_leaky", [P, 1]), sb("bn_shift_leaky", [P, 1])
        ident = sb("ident", [P, P])
        eps = sb("eps", [P, 1])
        raw = sb("edges_raw", [P, 3, T], I32)
        key = sb("edges_key", [P, 2, T])
        eidx = sb("edges_index", [P, 2, T], I32)
        row = sb("edges_row", [P, 2, T])
        col = sb("edges_col", [P, 2, T])
        tmpi = sb("tmp_int", [P, 2, 2, T], I32)
        later = sb("later_same_target", [P, 2, T])
        final = sb("last_of_group", [P, 2, T])
        latg = sb("later_slot", [P, M, K])
        latn = sb("later_next_slot", [P, M, K])
        sidxt = sb("scatter_index", [P, 2, T], I32)
        trash_i = sb("trash_int", [P, T], I32)
        trash = sb("trash", [P, T])
        tgt = sb("target", [P, T])
        typm = sb("type_mask", [P, R, T])
        from_mask = sb("from_mask", [P, K * P])
        scr = sb("scratch", [P, TT * P])
        ci = sb("column_int", [P, 2 * HC], I32)
        ch = sb("column_half", [P, 2 * HC], F16)
        ohp = sb("onehot_row", [P, U, P], F16)
        ohc = sb("onehot_col", [P, U, 2 * HC], F16)
        cS, cD = sb("rsqrt_deg_src", [P, 2 * HC]), sb("rsqrt_deg_dst", [P, 2 * HC])
        dg3, rd3, rd3sq = (sb(n, [P, 2 * HC]) for n in ("deg_in", "recip_deg_in", "recip_deg_in_squared"))
        both = dict(six=sb("bn_six", [P, U, 2 * G, 6]),
                    **{n: sb(n, [P, U, 2 * G]) for n in ("mean2", "diff", "var", "sd", "rs", "mean", "shift")})
        norm = {n: a[:, :, 0:G] for n, a in both.items()}
        bns = sb("bn_stats_all", [P, 2 * (NB - 1) + G, 6])
        bnm = sb("bn_mean_var", [P, 2])
        bnt = sb("bn_tmp", [P, 4])

        ps = ctx.enter_context(nc.psum_tensor("ps", [P, 8, 512], F32))

        def pair(i):
            return ps[:, 2 * i:2 * i + 2, :].rearrange("p a (h f) -> p (a h) f", f=D)

        def pair_flat(i):
            return ps[:, 2 * i:2 * i + 2, :].rearrange("p a e -> p (a e)")

        def sums_of(layer, q):
            if layer == 4:
                return ps[:, 2, 0:K * D].rearrange("p (k f) -> p k f", k=K)
            return ps[:, 2 + q % 2 * K:2 + (q % 2 + 1) * K, 0:D]

        def g3(a):
            return a.rearrange("p (g f) -> p g f", g=G)

        def per_node(table, b):
            return table[:, bass.ds(b * G, G)].unsqueeze(2).to_broadcast([P, G, D])

        def per_feature(r):
            return r[:, :].unsqueeze(1).to_broadcast([P, G, D])

        def known(v):
            return isinstance(v, int)

        def wait(eng, s, v):
            if not known(v) or v > 0:
                eng.wait_ge(s, v)

        def steps(eng, n, skew, body, slots=U):
            head = min(n, slots * -(-(skew + slots) // slots))
            rounds = (n - head) // slots
            for t in range(head):
                body(t, t % slots, lambda b: 0 <= b < n)
            if rounds:
                with eng.Fori(0, rounds) as i:
                    for u in range(slots):
                        body(i * slots + (head + u), u, lambda b: True)
            for t in range(head + rounds * slots, n + skew):
                body(t, t % slots, lambda b: 0 <= b < n)

        def nth(j, b, s, n=NB, unit=16, slots=U):
            return j * -(-(n - s) // slots) * unit + (b - s) * (unit // slots) + unit

        def all_through(eng, ring, j, n=NB, unit=16, slots=U):
            for s in range(slots):
                eng.wait_ge(ring[s], (j + 1) * -(-(n - s) // slots) * unit)

        def freed(eng, ring, j, b, s, n=NB, unit=16, slots=U):
            if not known(b) or b >= slots:
                eng.wait_ge(ring[s], nth(j, b - slots, s, n, unit, slots))

        def group(layer, b, s):
            return nth(layer, b, s, NG, 16 * K, UE)

        def group_freed(eng, ring, layer, b, s):
            freed(eng, ring, layer, b, s, NG, 16 * K, UE)

        def all_groups(eng, ring, layer):
            all_through(eng, ring, layer, NG, 16 * K, UE)

        def at(layer):
            return dict(targets=1, matrices=2, sums=4) if layer < 4 else dict(
                gT=3, gT_in=4, targets=5, relations=5, matrices=6, first_type=6, other_types=7, sums=8)

        def sems(name, slots=U):
            return [sem(f"{name}_{s}") for s in range(slots)]

        zin_in, xin_in, z_stored, x_stored = sems("zin_in"), sems("xin_in"), sems("z_stored"), sems("x_stored")
        raw_zero = sem("raw_zero")
        consts_in = sem("consts_in")
        N_CONST = 15 + 6
        pool_consts = sem("pool_consts")
        pchain = sem("pool_chain")
        keys_raw = sem("keys_raw")
        keys_padded = sem("keys_padded")
        prep = sem("vector_prep_chain")
        onehot = sem("onehot")
        hist_used = sem("hist_used")
        deg1 = sem("deg_plus_one")
        deg_sqrt = sem("deg_sqrt")
        wT_ps, wT_sb = sem("weights_T_psum"), sem("weights_T_sbuf")
        last_table, lat_table = sem("last_table"), sem("later_table")
        prep_done = sem("prep_done")
        zeros_in = sem("trash_zeroed")
        deg_ready = sem("degrees_ready")
        targets = sem("scatter_indices_ready")
        key_slot = sem("key_slot_in")
        begun = sem("indirect_group_begun")

        gidx_in = sem("gather_index_in")
        gathered = sems("gathered", UE)
        keyR = sem("keyR")
        same_in = sem("same_in")
        grouped = sem("grouped")
        msg_in = sem("message_in")
        sca_in = sem("scatter_rows_in")
        scattered = sems("scattered", UE)
        gatT_ps, gatT_sb, rel_ps, rel_in, rel_chain = (sem(n) for n in (
            "gatheredT_psum", "gatheredT_sbuf", "relations_psum", "relation_msg_in", "relation_chain"))

        def node_pass(name, names, zl=0, xl=0, zs=0, xs=0):
            return dict(zl=zl, xl=xl, zs=zs, xs=xs, **{n: sem(f"{name}_{n}") for n in names.split()})

        p0 = node_pass("p0", "x_T xT_in proj biased z_out", xl=0, zs=0)
        p1 = node_pass("p1", "v ua dva var sd dvb x_out x_T xT_in proj z_out", zl=0, xl=1, zs=1, xs=0)
        p2 = node_pass("p2", "v x_T xT_in proj z_out", zl=1, zs=2)
        p3 = node_pass("p3", "v v_chain ua dva var sd dvb x_out x_T xT_in proj z_out", zl=2, xl=2, zs=3, xs=1)
        p4 = node_pass("p4", "v v_high x_T stats", zl=3)
        p5 = node_pass("p5", "v v_T hT leaky h_back ua dva var sd dvb x_out x_T xT_in proj z_out",
                       zl=4, xl=3, zs=4, xs=2)
        p6 = node_pass("p6", "stats stats2 sums squares raw_var var sd scale scaled fin y gam xb ua o_low o_out", xs=3)
        zin6_in, xin6_in = sems("zin_last_in", UL), sems("xin_last_in", UL)
        LOW = 3
        LAG = 6
        bn_chain, bn_sd, bn_ready = sem("bn_chain"), sem("bn_sd"), sem("bn_ready")

        block = ctx.enter_context(nc.Block())

        def after_p0(e):
            all_through(e, z_stored, p0["zs"])

        def after_edges(e, layer):
            all_groups(e, scattered, layer)

        def after_p1(e):
            all_through(e, z_stored, p1["zs"])
            all_through(e, x_stored, p1["xs"])

        def after_p2(e):
            all_through(e, z_stored, p2["zs"])

        def after_p3(e):
            all_through(e, z_stored, p3["zs"])
            all_through(e, x_stored, p3["xs"])

        def after_p5(e):
            all_through(e, z_stored, p5["zs"])
            all_through(e, x_stored, p5["xs"])

        @block.sync
        def _(sp):
            for a, s in ((W0n, W0), (Wln, Wl), (W1s, W1), (W2s, W2), (W3s, W3)):
                sp.dma_start(a[:, :], s[:, :]).then_inc(consts_in, 16)
            sp.dma_start(Wrs[:, :].rearrange("i (r o) -> i r o", r=R),
                         Wr.rearrange("r i o -> i r o")).then_inc(consts_in, 16)
            for a, s in ((b0B, b0), (b2B, b2), (blB, bl), (g4B, gam4), (e4B, bet4)):
                sp.dma_start(a[:, :], s.unsqueeze(0).to_broadcast([P, D])).then_inc(consts_in, 16)
            for a, s in ((b1C, b1), (b3C, b3), (g3C, gam3), (e3C, bet3)):
                sp.dma_start(a[:, :], s.rearrange("(p o) -> p o", o=1)).then_inc(consts_in, 16)
            sp.wait_ge(raw_zero, 1)
            for i, s in enumerate((src, dst, edge_type)):
                sp.dma_start(raw[0:EFULL, i, :], s[0:EFULL * T].rearrange("(p t) -> p t", t=T)).then_inc(consts_in, 16)
                sp.dma_start(raw[EFULL:EFULL + 1, i, 0:EREST], s[EFULL * T:E].unsqueeze(0)).then_inc(consts_in, 16)
            sp.dma_start(Z[NP:NP + TRASH, :].rearrange("(p k) f -> p (k f)", k=TT), scr[:, :]).then_inc(zeros_in, 16)

            def load_x(b, s, free, from_input):
                wait(sp, free, b - U + 1)
                if from_input and known(b) and b == NB - 1:
                    sp.dma_start(xin[0:LASTP, s, :], x_last).then_inc(xin_in[s], 16)
                else:
                    sp.dma_start(xin[:, s, :], (x_full if from_input else Xb)[b]).then_inc(xin_in[s], 16)

            def load_z(b, s, free):
                wait(sp, free, b - U + 1)
                sp.dma_start(zin[:, s, :], Zb[b]).then_inc(zin_in[s], 16)

            def load_steps(body):
                steps(sp, NB, 1, lambda t, s, live: body(t - 1, (s - 1) % U) if live(t - 1) else None)

            load_steps(lambda b, s: load_x(b, s, p0["x_T"], True))
            after_edges(sp, 0)

            def p1_loads(b, s):
                load_z(b, s, p1["v"])
                load_x(b, s, p1["var"], True)
            load_steps(p1_loads)
            after_edges(sp, 1)
            load_steps(lambda b, s: load_z(b, s, p2["v"]))
            after_edges(sp, 2)

            def p3_loads(b, s):
                load_z(b, s, p3["v"])
                load_x(b, s, p3["var"], False)
            load_steps(p3_loads)
            after_edges(sp, 3)
            
            def p4_loads(b, s):
                wait(sp, p4["v_high"], b - U + 1)
                load_z(b, s, p4["v"])
            load_steps(p4_loads)
            sp.wait_ge(p4["v"], NB)
            sp.wait_ge(p4["v_high"], NB)

            def p5_loads(t, s, live):
                if live(t):
                    load_z(t, s, p5["v"])
                if live(t - 4):
                    load_x(t - 4, s, p5["x_out"], False)
            steps(sp, NB, 4, p5_loads)
            after_edges(sp, 4)

            def p6_loads(t, s, live):
                if live(t):
                    wait(sp, p6["y"], t - UL + 1)
                    sp.dma_start(zin6[:, s, :], Zb[t]).then_inc(zin6_in[s], 16)
                if live(t - 3):
                    b, q = t - 3, (s - 3) % UL
                    wait(sp, p6["ua"], b - UL + 1)
                    sp.dma_start(xin6[:, q, :], Xb[b]).then_inc(xin6_in[q], 16)
            steps(sp, NB, 3, p6_loads, UL)
            sp.wait_ge(zeros_in, 16)
            all_through(sp, x_stored, p6["xs"])

        @block.gpsimd
        def _(pool):
            n = [0]

            def link(ins):
                n[0] += 1
                ins.then_inc(pchain, 1)
                pool.wait_ge(pchain, n[0])

            link(nc.gpsimd.memset(ident[:, :], 0.0))
            link(nc.gpsimd.affine_select(out=ident[:, :], in_=ident[:, :], compare_op=ALU.not_equal, fill=1.0, base=0,
                                         pattern=[[-1, P]], channel_multiplier=1))
            link(nc.gpsimd.memset(from_mask[:, :], 1.0))
            link(nc.gpsimd.affine_select(out=from_mask[:, 0:P], in_=from_mask[:, 0:P], compare_op=ALU.is_ge, fill=0.0,
                                         base=0, pattern=[[1, P]], channel_multiplier=-1))
            nc.gpsimd.iota(trash_i[:, :], pattern=[[0, T // TT], [P, TT]], base=NP, channel_multiplier=1)
            nc.gpsimd.iota(ci[:, :], pattern=[[1, 2 * HC]], base=0, channel_multiplier=0).then_inc(pool_consts, 1)
            pool.wait_ge(keys_raw, 1)
            for i in range(2):
                last = nc.gpsimd.affine_select(out=key[:, i, :], in_=key[:, i, :], compare_op=ALU.is_ge,
                                               fill=float(N), base=E - 1, pattern=[[-1, T]], channel_multiplier=-T)
            last.then_inc(keys_padded, 1)

            def gather(layer, table, rows):
                def body(t, s, live):
                    base = layer * NG
                    wait(pool, gidx_in, base + t + 1)
                    if layer < 4:
                        wait(pool, grouped, base + t - UE + 1)
                    else:
                        wait(pool, gatT_ps, t - UE + 1)
                    pool.sem_inc(begun, 1)
                    for k in range(K):
                        nc.gpsimd.indirect_dma_start(
                            out=gat[:, s, k * D:(k + 1) * D], out_offset=None, in_=rows,
                            in_offset=bass.IndirectOffsetOnAxis(ap=gidx[:, s, k:k + 1], axis=0)).then_inc(gathered[s], 16)
                steps(pool, NG, 0, body, UE)

            def scatter(layer):
                all_groups(pool, gathered, layer)
                if layer == 0:
                    pool.wait_ge(zeros_in, 16)

                def body(t, s, live):
                    base = layer * NG
                    wait(pool, sca_in, base + t + 1)
                    if not known(t) or t >= 2:
                        q = (s - 2) % UE
                        pool.wait_ge(scattered[q], group(layer, t - 2, q))
                    pool.sem_inc(begun, 1)
                    for k in range(K):
                        nc.gpsimd.indirect_dma_start(
                            out=Z[:, :], out_offset=bass.IndirectOffsetOnAxis(ap=sidx[:, s, k:k + 1], axis=0),
                            in_=sca[:, s, k * D:(k + 1) * D], in_offset=None,
                            compute_op=ALU.add).then_inc(scattered[s], 16)
                steps(pool, NG, 0, body, UE)

            def scale(q, b, s, table, free):
                pool.wait_ge(zin_in[s], nth(q["zl"], b, s))
                wait(pool, free, b - U + 1)
                nc.gpsimd.tensor_tensor(g3(vv[:, s, :]), g3(zin[:, s, :]), per_node(table, b),
                                        ALU.mult).then_inc(q["v"], 1)

            after_p0(pool)
            gather(0, 1, Z[:, :])
            scatter(0)
            steps(pool, NB, 0, lambda t, s, live: scale(p1, t, s, cS, p1["x_out"]))
            after_p1(pool)
            gather(1, 0, Z[:, :])
            scatter(1)
            steps(pool, NB, 0, lambda t, s, live: scale(p2, t, s, cD, p2["x_T"]))
            after_p2(pool)
            gather(2, 0, Z[:, :])
            scatter(2)

            def p3_body(t, s, live):
                pool.wait_ge(zin_in[s], nth(p3["zl"], t, s))
                wait(pool, p3["x_out"], t - U + 1)
                nc.gpsimd.tensor_tensor(g3(vv[:, s, :]), g3(zin[:, s, :]), per_node(cD, t),
                                        ALU.mult).then_inc(p3["v_chain"], 1)
                pool.wait_ge(p3["v_chain"], t + 1)
                nc.gpsimd.tensor_tensor(g3(vv[:, s, :]), g3(vv[:, s, :]), per_feature(b2B),
                                        ALU.add).then_inc(p3["v"], 1)
            steps(pool, NB, 0, p3_body)
            after_p3(pool)
            gather(3, 0, Z[:, :])
            scatter(3)

            def p4_body(t, s, live):
                pool.wait_ge(zin_in[s], nth(p4["zl"], t, s))
                wait(pool, p4["x_T"], t - U + 1)
                half = slice(0, ED // 2)
                nc.gpsimd.tensor_tensor(vv[:, s, half].rearrange("p (g f) -> p g f", f=D),
                                        zin[:, s, half].rearrange("p (g f) -> p g f", f=D),
                                        cD[:, bass.ds(t * G, G // 2)].unsqueeze(2).to_broadcast([P, G // 2, D]),
                                        ALU.mult).then_inc(p4["v"], 1)
            steps(pool, NB, 0, p4_body)
            pool.wait_ge(p4["x_T"], NB)

            def p5_body(t, s, live):
                if live(t - 3):
                    b, q = t - 3, (s - 3) % U
                    pool.wait_ge(p5["hT"], b + 1)
                    nc.gpsimd.tensor_tensor(hl[:, q, :], hl[:, q, :], vv[:, q, :], ALU.subtract).then_inc(p5["leaky"], 1)
                if live(t):
                    scale(p5, t, s, cD, p5["leaky"])
            steps(pool, NB, 3, p5_body)
            after_p5(pool)
            gather(4, 0, X[:, :])
            scatter(4)

            def p6_body(t, s, live):
                if live(t - 4):
                    b, q = t - 4, (s - 4) % UL
                    pool.wait_ge(p6["y"], b + 1)
                    nc.gpsimd.tensor_tensor(g3(zo6[:, q % U, :]), g3(zo6[:, q % U, :]), per_feature(g4B),
                                            ALU.mult).then_inc(p6["gam"], 1)
                    pool.wait_ge(xin6_in[q], nth(0, b, q, slots=UL))
                    nc.gpsimd.tensor_tensor(g3(xin6[:, q, :]), g3(xin6[:, q, :]), per_feature(e4B),
                                            ALU.add).then_inc(p6["xb"], 1)
            steps(pool, NB, 4, p6_body, UL)

        @block.scalar
        def _(act):
            act.wait_ge(wT_ps, 1)
            nc.scalar.activation(W0s[:, :], ps[:, 6, 0:D], ACT.Copy)
            nc.scalar.activation(Wls[:, :], ps[:, 6, D:2 * D], ACT.Copy).then_inc(wT_sb, 1)
            act.wait_ge(deg1, 1)
            nc.scalar.activation(cS[:, :], cS[:, :], ACT.Sqrt).then_inc(deg_sqrt, 1)

            def evac(q, b, s, func, bias):
                act.wait_ge(q["x_T"], b + 1)
                wait(act, q["proj"], b - U + 1)
                if bias is None:
                    bank = 2 if q is p5 else s % 2
                    nc.scalar.activation(xT[:, s, :], pair_flat(bank), func).then_inc(q["xT_in"], 1)
                else:
                    nc.scalar.activation(xT[:, s, :], pair_flat(s % 2), func, bias=bias).then_inc(q["xT_in"], 1)

            def root(q, b, s, norm, var_sem, sd_sem, free):
                act.wait_ge(var_sem, b + 1)
                wait(act, free, b - U + 1)
                nc.scalar.activation(norm["sd"][:, s, :], norm["var"][:, s, :], ACT.Sqrt, bias=eps[:, 0:1],
                                     scale=1.0 / D).then_inc(sd_sem, 1)

            def project_out(q, b, s, table, bank=None):
                act.wait_ge(q["proj"], b + 1)
                freed(act, z_stored, q["zs"], b, s)
                projected = pair(2 + s % 2 if bank is None else bank)
                for g in range(G):
                    last = nc.scalar.activation(zo[:, s, g * D:(g + 1) * D], projected[:, g, :], ACT.Copy,
                                                scale=table[:, bass.ds(b * G + g, 1)])
                last.then_inc(q["z_out"], 1)

            def store_z(q, b, s):
                act.wait_ge(q["z_out"], b + 1)
                act.dma_start(Zb[b], zo[:, s, :]).then_inc(z_stored[s], 16)

            def store_x(q, b, s):
                act.wait_ge(q["x_out"], b + 1)
                act.dma_start(Xb[b], xo[:, s, :]).then_inc(x_stored[s], 16)

            def edges(layer):
                base = layer * NG
                after = at(layer)

                def body(t, s, live):
                    if layer == 4 and live(t - after["gT_in"]):
                        b, q = t - after["gT_in"], (s - after["gT_in"]) % UE
                        act.wait_ge(gatT_ps, b + 1)
                        wait(act, rel_ps, b - M + 1)
                        nc.scalar.activation(gatT[:, q % M, :], ps[:, 3, 0:K * P], ACT.Copy).then_inc(gatT_sb, 1)
                    if layer == 4 and live(t - after["first_type"]):
                        b, q = t - after["first_type"], (s - after["first_type"]) % UE
                        act.wait_ge(rel_ps, b + 1)
                        wait(act, grouped, base + b - M + 1)
                        for k in range(K):
                            last = nc.scalar.activation(relmsg[:, q % M, k * D:(k + 1) * D],
                                                        ps[:, 4 + q % 2 * K + k, 0:D], ACT.Copy,
                                                        scale=typm[:, 0, bass.ds(b * K + k, 1)])
                        last.then_inc(rel_in, 1)
                    if live(t - after["sums"]):
                        b, q = t - after["sums"], (s - after["sums"]) % UE
                        act.wait_ge(grouped, base + b + 1)
                        nc.scalar.activation(messages[:, bass.ds(b, 1), :].rearrange("p a (k f) -> p (a k) f", k=K),
                                             sums_of(layer, q), ACT.Copy).then_inc(msg_in, 1)
                steps(act, NG, after["sums"], body, UE)
                all_groups(act, gathered, layer)
                act.wait_ge(msg_in, base + NG)
                act.wait_ge(targets, min(layer, 1) + 1)

                def copies(t, s, live):
                    group_freed(act, scattered, layer, t, s)
                    nc.scalar.activation(sidx[:, s, :], sidxt[:, min(layer, 1), bass.ds(t * K, K)], ACT.Copy)
                    nc.scalar.activation(sca[:, s, :], messages[:, bass.ds(t, 1), :].rearrange("p a e -> p (a e)"),
                                         ACT.Copy).then_inc(sca_in, 1)
                steps(act, NG, 0, copies, UE)

            def p0_body(t, s, live):
                if live(t - 3):
                    store_z(p0, t - 3, (s - 3) % U)
                if live(t):
                    evac(p0, t, s, ACT.Copy, None)
            act.wait_ge(prep_done, 1)
            steps(act, NB, 3, p0_body)
            after_p0(act)
            edges(0)
            act.wait_ge(deg1, 2)
            nc.scalar.activation(cD[:, :], cD[:, :], ACT.Sqrt).then_inc(deg_sqrt, 1)

            def mid(q, table):
                def body(t, s, live):
                    if live(t):
                        root(q, t, s, norm, q["var"], q["sd"], q["x_out"])
                    if live(t - 2):
                        evac(q, t - 2, (s - 2) % U, ACT.Copy, None)
                        store_x(q, t - 2, (s - 2) % U)
                    if live(t - 4):
                        project_out(q, t - 4, (s - 4) % U, table)
                        store_z(q, t - 4, (s - 4) % U)
                steps(act, NB, 4, body)
            after_edges(act, 0)
            act.wait_ge(deg_ready, 1)
            mid(p1, cD)
            after_p1(act)
            edges(1)
            after_edges(act, 1)

            def p2_body(t, s, live):
                if live(t):
                    evac(p2, t, s, ACT.Relu, b1C[:, 0:1])
                if live(t - 3):
                    store_z(p2, t - 3, (s - 3) % U)
            steps(act, NB, 3, p2_body)
            after_p2(act)
            edges(2)
            after_edges(act, 2)
            mid(p3, cS)
            after_p3(act)
            edges(3)
            after_edges(act, 3)

            def p4_body(t, s, live):
                act.wait_ge(zin_in[s], nth(p4["zl"], t, s))
                wait(act, p4["x_T"], t - U + 1)
                for g in range(G // 2, G):
                    last = nc.scalar.activation(vv[:, s, g * D:(g + 1) * D], zin[:, s, g * D:(g + 1) * D], ACT.Copy,
                                                scale=cD[:, bass.ds(t * G + g, 1)])
                last.then_inc(p4["v_high"], 1)
            steps(act, NB, 0, p4_body)
            act.wait_ge(bn_chain, 1)
            nc.scalar.activation(bnt[:, 0:1], bnm[:, 1:2], ACT.Sqrt, bias=eps[:, 0:1]).then_inc(bn_sd, 1)
            act.wait_ge(bn_ready, 1)

            def p5_body(t, s, live):
                if live(t - 9):
                    evac(p5, t - 9, (s - 9) % U, ACT.Copy, None)
                if live(t - 2):
                    b, q = t - 2, (s - 2) % U
                    act.wait_ge(p5["v_T"], b + 1)
                    wait(act, p5["h_back"], b - U + 1)
                    nc.scalar.activation(hl[:, q, :], pair_flat(0), ACT.Relu, bias=bnB[:, 0:1], scale=bnA[:, 0:1])
                    nc.scalar.activation(vv[:, q, :], pair_flat(0), ACT.Relu, bias=bnb[:, 0:1],
                                         scale=bna[:, 0:1]).then_inc(p5["hT"], 1)
                if live(t - 6):
                    root(p5, t - 6, (s - 6) % U, norm, p5["var"], p5["sd"], p5["x_out"])
                if live(t - 8):
                    store_x(p5, t - 8, s)
                if live(t - 11):
                    project_out(p5, t - 11, (s - 11) % U, dg3, 3)
                    store_z(p5, t - 11, (s - 11) % U)
            steps(act, NB, 11, p5_body)
            after_p5(act)
            edges(4)
            after_edges(act, 4)

            def p6_body(t, s, live):
                if live(t - 1) or live(t - 1 - LAG):
                    root(p6, t - 1, (s - 1) % U, both, p6["var"], p6["sd"], p6["fin"])
                if live(t - 3):
                    b, q = t - 3, (s - 3) % UL
                    act.wait_ge(p6["fin"], b + 1)
                    wait(act, p6["ua"], b - U + 1)
                    for g in range(G):
                        last = nc.scalar.activation(zo6[:, q % U, g * D:(g + 1) * D], zin6[:, q, g * D:(g + 1) * D],
                                                    ACT.Identity, bias=both["shift"][:, q % U, g:g + 1],
                                                    scale=both["rs"][:, q % U, g:g + 1])
                    last.then_inc(p6["y"], 1)
                if live(t - 8):
                    b, q = t - 8, (s - 8) % U
                    r = (s - 2) % U
                    act.wait_ge(p6["fin"], b + LAG + 1)
                    freed(act, x_stored, p6["xs"], b, q)
                    for g in (*range(G // 2, G), *range(LOW, G // 2)):
                        if g == LOW:
                            act.wait_ge(p6["o_low"], b + 1)
                        last = nc.scalar.activation(xo6[:, q, g * D:(g + 1) * D], pair(q)[:, g, :], ACT.Identity,
                                                    bias=both["shift"][:, r, G + g:G + g + 1],
                                                    scale=both["rs"][:, r, G + g:G + g + 1])
                    last.then_inc(p6["o_out"], 1)
                    act.wait_ge(p6["o_out"], b + 1)
                    if known(b) and b == NB - 1:
                        act.dma_start(out_last, xo6[0:LASTP, q, :]).then_inc(x_stored[q], 16)
                    else:
                        act.dma_start(out_full[b], xo6[:, q, :]).then_inc(x_stored[q], 16)
            steps(act, NB, 8, p6_body, UL)

        @block.vector
        def _(dve):
            n = [0]

            def link(ins):
                n[0] += 1
                ins.then_inc(prep, 1)
                dve.wait_ge(prep, n[0])

            nc.vector.memset(raw[:, :, :], 0)
            nc.vector.memset(eps[:, :], EPS)
            nc.vector.memset(latg[:, :, :], 0.0)
            nc.vector.memset(latn[:, :, :], 0.0)
            nc.vector.memset(scr[:, :], 0.0).then_inc(raw_zero, 1)
            dve.wait_ge(consts_in, 16 * N_CONST)
            nc.vector.tensor_copy(key[:, :, :], raw[:, 0:2, :]).then_inc(keys_raw, 1)
            for r in range(R):
                nc.vector.tensor_scalar(typm[:, r, :], raw[:, 2, :], float(r), None, ALU.is_equal)
            dve.wait_ge(pool_consts, 1)
            nc.vector.tensor_copy(trash[:, :], trash_i[:, :])
            nc.vector.tensor_copy(ch[:, :], ci[:, :])
            dve.wait_ge(keys_padded, 1)
            link(nc.vector.tensor_copy(eidx[:, :, :], key[:, :, :]))
            nc.vector.tensor_scalar(tmpi[:, 0, :, :], eidx[:, :, :], 3, P - 1, ALU.logical_shift_right,
                                    ALU.bitwise_and)
            nc.vector.tensor_scalar(tmpi[:, 1, :, :], eidx[:, :, :], 10, 3, ALU.logical_shift_right,
                                    ALU.logical_shift_left)
            link(nc.vector.tensor_copy(later[:, :, :], key[:, :, :]))
            link(nc.vector.tensor_copy(row[:, :, :], tmpi[:, 0, :, :]))
            link(nc.vector.tensor_copy(col[:, :, :], tmpi[:, 1, :, :]))
            link(nc.vector.tensor_scalar(tmpi[:, 0, :, :], eidx[:, :, :], G - 1, None, ALU.bitwise_and))
            link(nc.vector.tensor_copy(later[:, :, :], tmpi[:, 0, :, :]))
            link(nc.vector.tensor_tensor(col[:, :, :], col[:, :, :], later[:, :, :], ALU.add))

            def one_hots(i):
                def body(t, s, live):
                    wait(dve, hist_used, i * T + t - U + 1)
                    nc.vector.tensor_scalar(ohp[:, s, :], ch[:, 0:P], row[:, i, bass.ds(t, 1)], None, ALU.is_equal)
                    nc.vector.tensor_scalar(ohc[:, s, :], ch[:, :], col[:, i, bass.ds(t, 1)], None,
                                            ALU.is_equal).then_inc(onehot, 1)
                steps(dve, T, 0, body)
                dve.wait_ge(hist_used, (i + 1) * T)

            def hist(i):
                return ps[:, 4 + 2 * i:6 + 2 * i, 0:HC]

            def halves(a):
                return a[:, :].rearrange("p (a c) -> p a c", a=2)

            nc.vector.memset(ones[:, :], 1.0)
            nc.vector.memset(bl_rows[:, :], 0.0)
            link(nc.vector.tensor_copy(bl_parts[:, 0, :], blB[:, :]))
            link(nc.vector.tensor_tensor(bl_rest[:, 0, :], blB[:, :], bl_parts[:, 0, :], ALU.subtract))
            link(nc.vector.tensor_copy(bl_parts[:, 1, :], bl_rest[:, 0, :]))
            link(nc.vector.tensor_tensor(bl_rest[:, 1, :], bl_rest[:, 0, :], bl_parts[:, 1, :], ALU.subtract))
            link(nc.vector.tensor_copy(bl_parts[:, 2, :], bl_rest[:, 1, :]))
            for i in range(3):
                nc.vector.tensor_copy(bl_rows[32 * i:32 * i + 1, :], bl_parts[32 * i:32 * i + 1, i, :])

            one_hots(0)
            nc.vector.tensor_scalar(halves(cS), hist(0), 1.0, None, ALU.add).then_inc(deg1, 1)
            dve.wait_ge(deg_sqrt, 1)
            nc.vector.reciprocal(cS[:, :], cS[:, :]).then_inc(prep_done, 1)

            def dst_degrees():
                one_hots(1)
                nc.vector.tensor_scalar(halves(cD), hist(1), 1.0, None, ALU.add).then_inc(deg1, 1)
                link(nc.vector.tensor_scalar(halves(dg3), hist(1), 1.0, None, ALU.max))
                link(nc.vector.reciprocal(rd3[:, :], dg3[:, :]))
                nc.vector.tensor_tensor(rd3sq[:, :], rd3[:, :], rd3[:, :], ALU.mult)
                dve.wait_ge(deg_sqrt, 2)
                nc.vector.reciprocal(cD[:, :], cD[:, :]).then_inc(deg_ready, 1)

            def scatter_indices(i):
                dve.wait_ge(lat_table, (i + 1) * NG)
                link(nc.vector.tensor_scalar(later[:, i, :], later[:, i, :], -1.0, 1.0, ALU.add, ALU.min))
                link(nc.vector.tensor_tensor(tgt[:, :], trash[:, :], key[:, i, :], ALU.subtract))
                link(nc.vector.tensor_tensor(tgt[:, :], tgt[:, :], later[:, i, :], ALU.mult))
                link(nc.vector.tensor_tensor(tgt[:, :], tgt[:, :], key[:, i, :], ALU.add))
                nc.vector.tensor_copy(sidxt[:, i, :], tgt[:, :]).then_inc(targets, 1)

            def edges(layer, gi, ki):
                base = layer * NG

                after = at(layer)

                def settle(b, m):
                    dve.wait_ge(same_in, base + b + 1)
                    nc.vector.tensor_scalar(final[:, ki, bass.ds(b * K, K)], latg[:, m, :], 1.0, None,
                                            ALU.is_equal).then_inc(last_table, 1)
                    if not known(b) or b > 0:
                        nc.vector.tensor_tensor(later[:, ki, bass.ds((b - 1) * K, K)], latg[:, (m - 1) % M, :],
                                                latn[:, m, :], ALU.add).then_inc(lat_table, 1)
                    if known(b) and b == NG - 1:
                        nc.vector.tensor_copy(later[:, ki, b * K:T], latg[:, m, :]).then_inc(lat_table, 1)

                def body(t, s, live):
                    if layer == 4 and live(t - after["other_types"]):
                        b, q = t - after["other_types"], (s - after["other_types"]) % UE
                        dve.wait_ge(rel_in, b + 1)
                        for r in range(1, R):
                            if r > 1:
                                dve.wait_ge(rel_chain, b * (R - 1) + (r - 1))
                            for k in range(K):
                                m = relmsg[:, q % M, k * D:(k + 1) * D]
                                last = nc.vector.scalar_tensor_tensor(
                                    out=m, in0=ps[:, 4 + q % 2 * K + k, r * D:(r + 1) * D],
                                    scalar=typm[:, r, bass.ds(b * K + k, 1)], in1=m, op0=ALU.mult, op1=ALU.add)
                            last.then_inc(rel_chain, 1)
                    if live(t):
                        group_freed(dve, gathered, layer, t, s)
                        nc.vector.tensor_copy(gidx[:, s, :], eidx[:, gi, bass.ds(t * K, K)]).then_inc(gidx_in, 1)
                        wait(dve, keyR, base + t - UE + 1)
                        nc.vector.tensor_copy(kslot[:, s, :], key[:, ki, bass.ds(t * K, K)]).then_inc(key_slot, 1)
                    if live(t - after["matrices"]):
                        b, q = t - after["matrices"], (s - after["matrices"]) % UE
                        first = known(b) and b == 0
                        m = q % M
                        dve.wait_ge(keyR, base + b + 1)
                        wait(dve, grouped, base + b - M + 1)
                        for k in range(K):
                            mine = key[:, ki, bass.ds(b * K + k, 1)]
                            if layer > 1:
                                last = nc.vector.tensor_scalar(same[:, m, k, k * P:], ps[:, q % 2, k * P:K * P],
                                                               mine, None, ALU.is_equal)
                                continue
                            last = nc.vector.scalar_tensor_tensor(
                                out=same[:, m, k, k * P:], in0=ps[:, q % 2, k * P:K * P], scalar=mine,
                                in1=from_mask[:, 0:(K - k) * P], op0=ALU.is_equal, op1=ALU.mult,
                                accum_out=latg[:, m, k:k + 1])
                            if k == 0 and not first:
                                settle(b - 1, (m - 1) % M)
                        if not first:
                            if layer <= 1:
                                dve.wait_ge(last_table, base + b)
                            for k in range(K):
                                its = key[:, ki, bass.ds((b - 1) * K + k, 1)]
                                flag = final[:, ki, bass.ds((b - 1) * K + k, 1)]
                                if layer > 1:
                                    last = nc.vector.tensor_scalar(carry[:, m, k, :], ps[:, q % 2, 0:K * P], its,
                                                                   flag, ALU.is_equal, ALU.mult)
                                else:
                                    last = nc.vector.scalar_tensor_tensor(
                                        out=carry[:, m, k, :], in0=ps[:, q % 2, 0:K * P], scalar=its,
                                        in1=flag.to_broadcast([P, K * P]), op0=ALU.is_equal, op1=ALU.mult,
                                        accum_out=latn[:, m, k:k + 1])
                        last.then_inc(same_in, 1)
                        if layer <= 1 and known(b) and b == NG - 1:
                            settle(b, m)
                steps(dve, NG, after["other_types"] if layer == 4 else after["matrices"], body, UE)

            def ln_stats(a, b, s, norm, chain, done):
                six, mean2, diff, var = norm["six"], norm["mean2"], norm["diff"], norm["var"]
                for g in range(G):
                    last = nc.vector.bn_stats(six[:, s, g, :], a[:, g, :])
                last.then_inc(chain, 1)
                dve.wait_ge(chain, b * 3 + 1)
                nc.vector.tensor_tensor(diff[:, s, :], six[:, s, :, 1], six[:, s, :, 4], ALU.subtract)
                nc.vector.tensor_tensor(mean2[:, s, :], six[:, s, :, 1], six[:, s, :, 4], ALU.add)
                nc.vector.tensor_tensor(var[:, s, :], six[:, s, :, 2], six[:, s, :, 5], ALU.add).then_inc(chain, 1)
                dve.wait_ge(chain, b * 3 + 2)
                nc.vector.tensor_tensor(diff[:, s, :], diff[:, s, :], diff[:, s, :], ALU.mult)
                nc.vector.tensor_scalar(norm["mean"][:, s, :], mean2[:, s, :], 0.5, None, ALU.mult).then_inc(chain, 1)
                dve.wait_ge(chain, b * 3 + 3)
                nc.vector.scalar_tensor_tensor(out=var[:, s, :], in0=diff[:, s, :], scalar=D / 4.0, in1=var[:, s, :],
                                               op0=ALU.mult, op1=ALU.add).then_inc(done, 1)

            def norm_out(q, b, s, a=vv):
                dve.wait_ge(q["sd"], b + 1)
                nc.vector.reciprocal(norm["rs"][:, s, :], norm["sd"][:, s, :]).then_inc(q["dvb"], 1)
                wait(dve, q["x_T"], b - U + 1)
                freed(dve, x_stored, q["xs"], b, s)
                dve.wait_ge(q["dvb"], b + 1)
                for g in range(G):
                    last = nc.vector.tensor_scalar(xo[:, s, g * D:(g + 1) * D], a[:, s, g * D:(g + 1) * D],
                                                   norm["mean"][:, s, g:g + 1], norm["rs"][:, s, g:g + 1],
                                                   ALU.subtract, ALU.mult)
                last.then_inc(q["x_out"], 1)

            def biased(q, b, s, bias, bank):
                dve.wait_ge(q["proj"], b + 1)
                freed(dve, z_stored, q["zs"], b, s)
                nc.vector.tensor_tensor(g3(zo[:, s, :]), pair(bank), per_feature(bias), ALU.add).then_inc(q["biased"], 1)

            def p0_body(t, s, live):
                biased(p0, t, s, b0B, 2 + s % 2)
                dve.wait_ge(p0["biased"], t + 1)
                nc.vector.tensor_tensor(g3(zo[:, s, :]), g3(zo[:, s, :]), per_node(cS, t), ALU.mult).then_inc(p0["z_out"], 1)
            steps(dve, NB, 0, p0_body)
            after_p0(dve)
            edges(0, 1, 0)
            scatter_indices(0)
            dst_degrees()
            after_edges(dve, 0)

            def p1_body(t, s, live):
                if live(t):
                    dve.wait_ge(p1["v"], t + 1)
                    dve.wait_ge(xin_in[s], nth(p1["xl"], t, s))
                    nc.vector.scalar_tensor_tensor(out=vv[:, s, :], in0=vv[:, s, :], scalar=0.0, in1=xin[:, s, :],
                                                   op0=ALU.max, op1=ALU.add).then_inc(p1["ua"], 1)
                    dve.wait_ge(p1["ua"], t + 1)
                    ln_stats(g3(vv[:, s, :]), t, s, norm, p1["dva"], p1["var"])
                if live(t - 1):
                    norm_out(p1, t - 1, (s - 1) % U)
            steps(dve, NB, 1, p1_body)
            after_p1(dve)
            edges(1, 0, 1)
            scatter_indices(1)
            after_edges(dve, 1)

            def p2_body(t, s, live):
                dve.wait_ge(p2["proj"], t + 1)
                freed(dve, z_stored, p2["zs"], t, s)
                nc.vector.tensor_tensor(g3(zo[:, s, :]), pair(2 + s % 2), per_node(cD, t),
                                        ALU.mult).then_inc(p2["z_out"], 1)
            steps(dve, NB, 0, p2_body)
            after_p2(dve)
            edges(2, 0, 1)
            after_edges(dve, 2)

            def p3_body(t, s, live):
                if live(t):
                    dve.wait_ge(p3["v"], t + 1)
                    dve.wait_ge(xin_in[s], nth(p3["xl"], t, s))
                    nc.vector.tensor_tensor(vv[:, s, :], vv[:, s, :], xin[:, s, :], ALU.add).then_inc(p3["ua"], 1)
                    dve.wait_ge(p3["ua"], t + 1)
                    ln_stats(g3(vv[:, s, :]), t, s, norm, p3["dva"], p3["var"])
                if live(t - 1):
                    norm_out(p3, t - 1, (s - 1) % U)
            steps(dve, NB, 1, p3_body)
            after_p3(dve)
            edges(3, 0, 1)
            after_edges(dve, 3)

            def p4_body(t, s, live):
                dve.wait_ge(p4["x_T"], t + 1)
                if known(t) and t == NB - 1:
                    for g in range(G):
                        last = nc.vector.bn_stats(bns[:, 2 * (NB - 1) + g, :], pair(s)[:, g, 0:LASTP])
                else:
                    for h in range(2):
                        last = nc.vector.bn_stats(bns[:, bass.ds(t * 2 + h, 1), :].rearrange("p a e -> p (a e)"),
                                                  ps[:, 2 * s + h, :])
                last.then_inc(p4["stats"], 1)
            steps(dve, NB - 1, 0, p4_body)
            p4_body(NB - 1, (NB - 1) % U, None)
            dve.wait_ge(p4["stats"], NB)
            nc.vector.bn_aggr(bnm[:, :], bns[:, :, :].rearrange("p a e -> p (a e)")).then_inc(bn_chain, 1)
            dve.wait_ge(bn_chain, 1)
            nc.vector.tensor_tensor(bnt[:, 1:2], bnm[:, 0:1], b3C[:, :], ALU.add).then_inc(bn_chain, 1)
            dve.wait_ge(bn_sd, 1)
            nc.vector.reciprocal(bnt[:, 2:3], bnt[:, 0:1]).then_inc(bn_chain, 1)
            dve.wait_ge(bn_chain, 3)
            nc.vector.tensor_tensor(bnA[:, :], bnt[:, 2:3], g3C[:, :], ALU.mult).then_inc(bn_chain, 1)
            nc.vector.tensor_tensor(bnt[:, 3:4], b3C[:, :], bnt[:, 1:2], ALU.subtract).then_inc(bn_chain, 1)
            dve.wait_ge(bn_chain, 5)
            nc.vector.tensor_tensor(bnB[:, :], bnt[:, 3:4], bnA[:, :], ALU.mult).then_inc(bn_chain, 1)
            dve.wait_ge(bn_chain, 6)
            nc.vector.tensor_tensor(bnB[:, :], bnB[:, :], e3C[:, :], ALU.add).then_inc(bn_chain, 1)
            dve.wait_ge(bn_chain, 7)
            nc.vector.tensor_scalar(bna[:, :], bnA[:, :], -0.01, None, ALU.mult)
            nc.vector.tensor_scalar(bnb[:, :], bnB[:, :], -0.01, None, ALU.mult).then_inc(bn_ready, 1)

            def p5_body(t, s, live):
                b, q = t - 5, (s - 5) % U
                c, r = t - 7, (s - 7) % U
                six, mean2, diff, var = (norm[n][:, q] for n in ("six", "mean2", "diff", "var"))

                def normalise(part):
                    for g in part:
                        last = nc.vector.tensor_scalar(xo[:, r, g * D:(g + 1) * D], xin[:, r, g * D:(g + 1) * D],
                                                       norm["mean"][:, r, g:g + 1], norm["rs"][:, r, g:g + 1],
                                                       ALU.subtract, ALU.mult)
                    return last
                if live(b):
                    dve.wait_ge(p5["h_back"], b + 1)
                    dve.wait_ge(xin_in[q], nth(p5["xl"], b, q))
                    nc.vector.tensor_tensor(g3(xin[:, q, :]), pair(1), g3(xin[:, q, :]), ALU.add).then_inc(p5["ua"], 1)
                if live(c):
                    dve.wait_ge(p5["sd"], c + 1)
                    nc.vector.reciprocal(norm["rs"][:, r, :], norm["sd"][:, r, :]).then_inc(p5["dvb"], 1)
                if live(b):
                    dve.wait_ge(p5["ua"], b + 1)
                    for g in range(G):
                        last = nc.vector.bn_stats(six[:, g, :], xin[:, q, g * D:(g + 1) * D])
                    last.then_inc(p5["dva"], 1)
                if live(c):
                    wait(dve, p5["x_T"], c - U + 1)
                    freed(dve, x_stored, p5["xs"], c, r)
                    dve.wait_ge(p5["dvb"], c + 1)
                    normalise(range(0, 4))
                if live(b):
                    dve.wait_ge(p5["dva"], b * 3 + 1)
                    nc.vector.tensor_tensor(diff, six[:, :, 1], six[:, :, 4], ALU.subtract)
                    nc.vector.tensor_tensor(mean2, six[:, :, 1], six[:, :, 4], ALU.add)
                    nc.vector.tensor_tensor(var, six[:, :, 2], six[:, :, 5], ALU.add).then_inc(p5["dva"], 1)
                if live(c):
                    normalise(range(4, 6))
                if live(b):
                    dve.wait_ge(p5["dva"], b * 3 + 2)
                    nc.vector.tensor_tensor(diff, diff, diff, ALU.mult)
                    nc.vector.tensor_scalar(norm["mean"][:, q, :], mean2, 0.5, None, ALU.mult).then_inc(p5["dva"], 1)
                if live(c):
                    normalise(range(6, 8)).then_inc(p5["x_out"], 1)
                if live(b):
                    dve.wait_ge(p5["dva"], b * 3 + 3)
                    nc.vector.scalar_tensor_tensor(out=var, in0=diff, scalar=D / 4.0, in1=var,
                                                   op0=ALU.mult, op1=ALU.add).then_inc(p5["var"], 1)
            steps(dve, NB, 7, p5_body)
            after_p5(dve)
            edges(4, 0, 1)
            after_edges(dve, 4)

            nc.vector.memset(both["six"][:, :, :, :], 0.0).then_inc(p6["scale"], 1)
            dve.wait_ge(p6["scale"], 1)

            def p6_body(t, s, live):
                def rounds(i):
                    return live(i) or live(i - LAG)

                i, r = t - 2, (s - 2) % U
                if rounds(i):
                    dve.wait_ge(p6["sd"], i + 1)
                    if live(i - U):
                        wait(dve, p6["y"], i - U + 1)
                    wait(dve, p6["o_out"], i - LAG - U + 1)
                    nc.vector.reciprocal(both["rs"][:, r, :], both["sd"][:, r, :]).then_inc(p6["scale"], 1)
                q = s % U
                if live(t):
                    dve.wait_ge(zin6_in[s], nth(0, t, s, slots=UL))
                    for g in range(G):
                        last = nc.vector.bn_stats(both["six"][:, q, g, :], zin6[:, s, g * D:(g + 1) * D])
                    last.then_inc(p6["stats"], 1)
                if live(i):
                    dve.wait_ge(p6["scale"], i + 2)
                    nc.vector.tensor_tensor(both["rs"][:, r, 0:G], both["rs"][:, r, 0:G], rd3[:, bass.ds(i * G, G)],
                                            ALU.mult).then_inc(p6["scaled"], 1)
                if live(t - LAG):
                    b = t - LAG
                    dve.wait_ge(p6["ua"], b + 1)
                    for g in range(G):
                        last = nc.vector.bn_stats(both["six"][:, q, G + g, :], pair((s - LAG) % U)[:, g, :])
                    last.then_inc(p6["stats2"], 1)
                if rounds(i):
                    dve.wait_ge(p6["scale"], i + 2)
                    if live(i):
                        dve.wait_ge(p6["scaled"], i + 1)
                    nc.vector.scalar_tensor_tensor(out=both["shift"][:, r, :], in0=both["mean2"][:, r, :], scalar=-0.5,
                                                   in1=both["rs"][:, r, :], op0=ALU.mult,
                                                   op1=ALU.mult).then_inc(p6["fin"], 1)
                six = both["six"]
                mean2, diff, var = (both[n][:, q, :] for n in ("mean2", "diff", "var"))
                if rounds(t):
                    if live(t):
                        dve.wait_ge(p6["stats"], t + 1)
                    if live(t - LAG):
                        dve.wait_ge(p6["stats2"], t - LAG + 1)
                    nc.vector.tensor_tensor(diff, six[:, q, :, 1], six[:, q, :, 4], ALU.subtract)
                    nc.vector.tensor_tensor(mean2, six[:, q, :, 1], six[:, q, :, 4], ALU.add)
                    nc.vector.tensor_tensor(var, six[:, q, :, 2], six[:, q, :, 5], ALU.add).then_inc(p6["sums"], 1)

                def low_nodes(part):
                    b, q = t - 8, s % U
                    dve.wait_ge(p6["fin"], b + LAG + 1)
                    freed(dve, x_stored, p6["xs"], b, q)
                    for g in part:
                        last = nc.vector.tensor_scalar(xo6[:, q, g * D:(g + 1) * D], pair(q)[:, g, :],
                                                       both["rs"][:, r, G + g:G + g + 1],
                                                       both["shift"][:, r, G + g:G + g + 1], ALU.mult, ALU.add)
                    return last
                if live(t - 8):
                    low_nodes(range(0, LOW - 1))
                if rounds(t):
                    dve.wait_ge(p6["sums"], t + 1)
                    nc.vector.tensor_tensor(diff, diff, diff, ALU.mult).then_inc(p6["squares"], 1)
                if live(t - 8):
                    low_nodes(range(LOW - 1, LOW)).then_inc(p6["o_low"], 1)
                if rounds(t):
                    dve.wait_ge(p6["squares"], t + 1)
                    last = nc.vector.scalar_tensor_tensor(out=var, in0=diff, scalar=D / 4.0, in1=var,
                                                          op0=ALU.mult, op1=ALU.add)
                    if live(t):
                        last.then_inc(p6["raw_var"], 1)
                        dve.wait_ge(p6["raw_var"], t + 1)
                        last = nc.vector.tensor_tensor(var[:, 0:G], var[:, 0:G], rd3sq[:, bass.ds(t * G, G)], ALU.mult)
                    last.then_inc(p6["var"], 1)
            steps(dve, NB, 8, p6_body, UL)

        @block.tensor
        def _(pe):
            pe.wait_ge(consts_in, 16 * N_CONST)
            pe.wait_ge(pool_consts, 1)
            nc.tensor.transpose(ps[:, 6, 0:D], W0n[:, :], ident[:, :])
            nc.tensor.transpose(ps[:, 6, D:2 * D], Wln[:, :], ident[:, :]).then_inc(wT_ps, 1)

            def histogram(i):
                def count(t, s, first, final):
                    pe.wait_ge(onehot, i * T + t + 1)
                    for h in range(2):
                        last = nc.tensor.matmul(ps[:, 4 + 2 * i + h, 0:HC], ohp[:, s, :],
                                                ohc[:, s, h * HC:(h + 1) * HC], start=first, stop=final)
                    last.then_inc(hist_used, 1)
                for t in range(U):
                    count(t, t, t == 0, False)
                with pe.Fori(0, T // U - 2) as j:
                    for u in range(U):
                        count(j * U + (U + u), u, False, False)
                for t in range(T - U, T):
                    count(t, t % U, False, t == T - 1)
            histogram(0)

            def key_rows(s, bank, done):
                for k in range(K):
                    last = nc.tensor.transpose(ps[:, bank, k * P:(k + 1) * P],
                                               kslot[:, s, k:k + 1].to_broadcast([P, P]), ident[:, :])
                last.then_inc(done, 1)

            pe.wait_ge(prep_done, 1)

            def transpose_batch(a, bank, done):
                for g in range(G):
                    last = nc.tensor.transpose(pair(bank)[:, g, :], a[:, g * D:(g + 1) * D], ident[:, :])
                last.then_inc(done, 1)

            def project(q, b, s, weight, bank, free, lag):
                pe.wait_ge(q["xT_in"], b + 1)
                wait(pe, free, b - lag + 1)
                for g in range(G):
                    last = nc.tensor.matmul(pair(bank)[:, g, :], xT[:, s, g * D:(g + 1) * D], weight[:, :],
                                            start=True, stop=True)
                last.then_inc(q["proj"], 1)

            def edges(layer, ki):
                base = layer * NG
                after = at(layer)

                def body(t, s, live):
                    if live(t - after["sums"]):
                        b, q = t - after["sums"], (s - after["sums"]) % UE
                        if layer == 4:
                            pe.wait_ge(rel_chain, (b + 1) * (R - 1))
                            rows = relmsg[:, q % M, :]
                        else:
                            pe.wait_ge(gathered[q], group(layer, b, q))
                            rows = gat[:, q, :]
                        pe.wait_ge(same_in, base + b + 1)
                        first = known(b) and b == 0
                        if layer == 4:
                            wait(pe, msg_in, base + b)
                        else:
                            wait(pe, msg_in, base + b - 2 + 1)

                        def own(j):
                            for k in range(j + 1):
                                last = nc.tensor.matmul(sums_of(layer, q)[:, j, :],
                                                        same[:, q % M, k, j * P:(j + 1) * P],
                                                        rows[:, k * D:(k + 1) * D], start=k == 0, stop=first and k == j)
                            return last

                        def carried(j):
                            for k in range(K):
                                last = nc.tensor.matmul(sums_of(layer, q)[:, j, :],
                                                        carry[:, q % M, k, j * P:(j + 1) * P],
                                                        big[:, bass.ds(((b - 1) * K + k) * D, D)],
                                                        start=False, stop=k == K - 1)
                            return last
                        if layer == 4:
                            for j in range(K):
                                last = own(j)
                                if not first:
                                    last = carried(j)
                        else:
                            for j in range(K):
                                last = own(j)
                            if not first:
                                pe.wait_ge(msg_in, base + b)
                                for j in range(K):
                                    last = carried(j)
                        last.then_inc(grouped, 1)
                    if live(t - after["targets"]):
                        b, q = t - after["targets"], (s - after["targets"]) % UE
                        wait(pe, same_in, base + b - 2 + 1)
                        pe.wait_ge(key_slot, base + b + 1)
                        key_rows(q, q % 2, keyR)
                    if layer == 4 and live(t - after["relations"]):
                        b, q = t - after["relations"], (s - after["relations"]) % UE
                        pe.wait_ge(gatT_sb, b + 1)
                        wait(pe, rel_chain, (b - 1) * (R - 1))
                        for k in range(K):
                            last = nc.tensor.matmul(ps[:, 4 + q % 2 * K + k, 0:R * D], gatT[:, q % M, k * P:(k + 1) * P],
                                                    Wrs[:, :], start=True, stop=True)
                        last.then_inc(rel_ps, 1)
                    if layer == 4 and live(t - after["gT"]):
                        b, q = t - after["gT"], (s - after["gT"]) % UE
                        pe.wait_ge(gathered[q], group(layer, b, q))
                        wait(pe, gatT_sb, b)
                        for k in range(K):
                            last = nc.tensor.transpose(ps[:, 3, k * P:(k + 1) * P], gat[:, q, k * D:(k + 1) * D],
                                                       ident[:, :])
                        last.then_inc(gatT_ps, 1)
                steps(pe, NG, after["sums"], body, UE)

            def plain(q, a, weight, free):
                def body(t, s, live):
                    if live(t):
                        a(t, s)
                        wait(pe, q["xT_in"], t - 2 + 1)
                        transpose_batch(ring(q)[:, s, :], s % 2, q["x_T"])
                    if live(t - 2):
                        project(q, t - 2, (s - 2) % U, weight, 2 + s % 2, free, 2)
                steps(pe, NB, 2, body)

            def ring(q):
                return xin if q is p0 else vv if q is p2 else xo

            plain(p0, lambda t, s: pe.wait_ge(xin_in[s], nth(p0["xl"], t, s)), W0s, p0["biased"])
            after_p0(pe)
            edges(0, 0)
            histogram(1)
            after_edges(pe, 0)
            plain(p1, lambda t, s: pe.wait_ge(p1["x_out"], t + 1), W1s, p1["z_out"])
            after_p1(pe)
            edges(1, 1)
            after_edges(pe, 1)
            plain(p2, lambda t, s: pe.wait_ge(p2["v"], t + 1), W2s, p2["z_out"])
            after_p2(pe)
            edges(2, 1)
            after_edges(pe, 2)
            plain(p3, lambda t, s: pe.wait_ge(p3["x_out"], t + 1), W3s, p3["z_out"])
            after_p3(pe)
            edges(3, 1)
            after_edges(pe, 3)

            def p4_body(t, s, live):
                pe.wait_ge(p4["v"], t + 1)
                pe.wait_ge(p4["v_high"], t + 1)
                wait(pe, p4["stats"], t - U + 1)
                transpose_batch(vv[:, s, :], s, p4["x_T"])
            steps(pe, NB, 0, p4_body)
            pe.wait_ge(p4["stats"], NB)

            def p5_body(t, s, live):
                if live(t - 8):
                    pe.wait_ge(p5["x_out"], t - 8 + 1)
                    wait(pe, p5["xT_in"], t - 8)
                    transpose_batch(xo[:, s, :], 2, p5["x_T"])
                if live(t - 1):
                    b, q = t - 1, (s - 1) % U
                    pe.wait_ge(p5["v"], b + 1)
                    wait(pe, p5["hT"], b)
                    transpose_batch(vv[:, q, :], 0, p5["v_T"])
                if live(t - 4):
                    pe.wait_ge(p5["leaky"], t - 4 + 1)
                    wait(pe, p5["ua"], t - 4)
                    transpose_batch(hl[:, s, :], 1, p5["h_back"])
                if live(t - 10):
                    b, q = t - 10, (s - 10) % U
                    pe.wait_ge(p5["xT_in"], b + 1)
                    wait(pe, p5["z_out"], b)
                    for g in range(G):
                        if g % 4 == 0:
                            nc.tensor.matmul(ps[:, 6 + g // 4, :], ones[:, :],
                                             bl_rows[:, :].unsqueeze(1).to_broadcast([P, 4, D]), start=True, stop=False)
                        last = nc.tensor.matmul(pair(3)[:, g, :], xT[:, q, g * D:(g + 1) * D], Wls[:, :],
                                                start=False, stop=g % 4 == 3)
                    last.then_inc(p5["proj"], 1)
            steps(pe, NB, 10, p5_body)
            after_p5(pe)
            edges(4, 1)

            def p6_body(t, s, live):
                if live(t - 5):
                    b, q = t - 5, (s - 5) % UL
                    pe.wait_ge(p6["gam"], b + 1)
                    pe.wait_ge(p6["xb"], b + 1)
                    wait(pe, p6["o_out"], b - U + 1)
                    wait(pe, p6["o_low"], b - U + 1)
                    for h in range(2):
                        half = slice(h * ED // 2, (h + 1) * ED // 2)
                        for k, a in enumerate((zo6[:, q % U, half], xin6[:, q, half])):
                            last = nc.tensor.matmul(ps[:, 2 * (q % U) + h, :], ident[:, :], a, start=k == 0, stop=k == 1)
                    last.then_inc(p6["ua"], 1)
            steps(pe, NB, 5, p6_body, UL)


_INS = ['x', 'src', 'dst', 'edge_type_3', 'L0_gnn_W', 'L0_gnn_b', 'L1_gnn_W1', 'L1_gnn_b1', 'L1_gnn_W2', 'L1_gnn_b2',
        'L2_gnn_W', 'L2_gnn_b', 'L2_gnn_gamma', 'L2_gnn_beta', 'L3_gnn_relation_weights', 'L3_gnn_lin_w',
        'L3_gnn_lin_b', 'L3_gnn_ln_gamma', 'L3_gnn_ln_beta']


def kernel(**inputs):
    import numpy as _np
    import concourse.bacc as _bacc
    from concourse import mybir as _mybir
    from concourse.bass_utils import run_bass_kernel_spmd as _run

    nc = _bacc.Bacc("TRN2", target_bir_lowering=False, num_devices=1)
    arrays, args = {}, []
    for name in _INS:
        a = _np.ascontiguousarray(inputs[name])
        arrays[f"in_{name}_dram"] = a
        args.append(nc.dram_tensor(f"in_{name}_dram", a.shape, _mybir.dt.from_np(a.dtype), kind="ExternalInput").ap())
    args.append(nc.dram_tensor("out_dram", (N, D), F32, kind="ExternalOutput").ap())
    build(nc, *args)
    r = _run(nc, [arrays], core_ids=[0])
    return r.results[0]["out_dram"]
```
